# Optimizing a Trainium2 kernel written in Bass

```python
import numpy as np
import jax
import jax.numpy as jnp

def _softmax(x, axis=-1):
    return jax.nn.softmax(x, axis=axis)

def _gelu(x):
    return jax.nn.gelu(x, approximate=True)

def _silu(x):
    return jax.nn.silu(x)

def _sigmoid(x):
    return jax.nn.sigmoid(x)

def _layernorm(x, axis=-1, eps=1e-05):
    m = jnp.mean(x, axis=axis, keepdims=True)
    v = jnp.var(x, axis=axis, keepdims=True)
    return (x - m) / jnp.sqrt(v + eps)

def _scatter_add(tgt, idx, src, axis=0):
    return tgt.at[idx].add(src)

def _segment_sum(src, seg, n):
    return jax.ops.segment_sum(src, seg, n)
kernel_name = 'mk_xattn_seq_d2_seqx_r2_52de28'

def setup_inputs(seed: int=0):
    np.random.seed(seed)
    _w = jnp.asarray

    def _rec_inputs():
        import jax
        import jax.numpy as jnp
        _rk = jax.random.key(seed)
        x = 7.22e-05 + 1 * jax.random.normal(jax.random.fold_in(_rk, 1), (8, 512, 512), jnp.float32)
        _lenS = 512 - jax.random.randint(jax.random.fold_in(_rk, 7), (8,), 0, max(1, 512 // 4) + 1, jnp.int32)
        _lenS2 = 512 - jax.random.randint(jax.random.fold_in(_rk, 8), (8,), 0, max(1, 512 // 4) + 1, jnp.int32)
        _ctx_1024P = jax.random.normal(jax.random.fold_in(_rk, 11), (8, 16, 512), jnp.float32)
        _ctx_1024c = jax.random.dirichlet(jax.random.fold_in(_rk, 511), 0.3 * jnp.ones((16,), jnp.float32), (8, 512))
        _ctx_1024t = jnp.einsum('bsk,bkd->bsd', _ctx_1024c, _ctx_1024P)
        _ctx_1024t = _ctx_1024t * jax.lax.rsqrt(jnp.mean(jnp.square(_ctx_1024t)) + 1e-12) * 0.953939
        ctx_1024 = 4.13588e-05 + 0.999923 * (_ctx_1024t + 0.3 * jax.random.normal(jax.random.fold_in(_rk, 611), (8, 512, 512), jnp.float32))
        fside_Bx1xSxS2_0 = -1.47943e-05 + 1.00017 * jax.random.normal(jax.random.fold_in(_rk, 12), (8, 1, 512, 512), jnp.float32)
        _validS = jnp.arange(512)[None, :] < _lenS[:, None]
        _validS2 = jnp.arange(512)[None, :] < _lenS2[:, None]
        _causal = jnp.tril(jnp.ones((512, 512), dtype=bool))
        mask_Bx1x1xS2_ik0 = jnp.where(jnp.broadcast_to(_validS2[:, None, None, :], (8, 1, 1, 512)), 0, 1).astype(jnp.int32)
        mask_1x1xSxS_ik0 = jnp.where(jnp.broadcast_to(_validS[0:1, None, None, :], (1, 1, 512, 512)), 0, 1).astype(jnp.int32)
        return (x, ctx_1024, fside_Bx1xSxS2_0, mask_Bx1x1xS2_ik0, mask_1x1xSxS_ik0)
    x, ctx_1024, fside_Bx1xSxS2_0, mask_Bx1x1xS2_ik0, mask_1x1xSxS_ik0 = _rec_inputs()

    def _L0_xattn_setup():
        import jax, jax.numpy as jnp
        import numpy as np
        N_HEAD = 16
        D_IN = 512
        D_K = 64
        D_V = 64
        LN_EPS = 1e-06
        NEG_INF = -1000000000.0
        key = jax.random.key(seed)
        ks = jax.random.split(key, 11)
        B, L = (4, 1024)
        q = jax.random.normal(ks[0], (B, L, D_IN), dtype=jnp.float32)
        k = jax.random.normal(ks[1], (B, L, D_IN), dtype=jnp.float32)
        v = jax.random.normal(ks[2], (B, L, D_IN), dtype=jnp.float32)
        add_attn = jax.random.normal(ks[3], (B, 1, L, L), dtype=jnp.float32)
        mask = jax.random.randint(ks[4], (B, 1, 1, L), 0, 2, dtype=jnp.int32)
        s = 1.0 / np.sqrt(D_IN)
        w_q = jax.random.normal(ks[5], (D_IN, N_HEAD * D_K), dtype=jnp.float32) * s
        w_k = jax.random.normal(ks[6], (D_IN, N_HEAD * D_K), dtype=jnp.float32) * s
        w_v = jax.random.normal(ks[7], (D_IN, N_HEAD * D_V), dtype=jnp.float32) * s
        w_o = jax.random.normal(ks[8], (N_HEAD * D_V, D_IN), dtype=jnp.float32) * s
        ln_g = jnp.ones((D_IN,), dtype=jnp.float32)
        ln_b = jnp.zeros((D_IN,), dtype=jnp.float32)
        return {'q': q, 'k': k, 'v': v, 'add_attn': add_attn, 'mask': mask, 'w_q': w_q, 'w_k': w_k, 'w_v': w_v, 'w_o': w_o, 'ln_g': ln_g, 'ln_b': ln_b}
    _L0_xattn_all = _L0_xattn_setup()
    _L0_xattn_in = {k: v for k, v in _L0_xattn_all.items() if k in ('w_q', 'w_k', 'w_v', 'w_o', 'ln_g', 'ln_b')}
    del _L0_xattn_all

    def _L1_xattn_setup():
        import jax, jax.numpy as jnp
        import numpy as np
        DIM = 512
        HEADS = 16
        HEAD_DIM = DIM // HEADS
        NEG = -1e+30
        EPS = 1e-05

        def _linear(x, w, b):
            return jnp.einsum('bnd,od->bno', x, w) + b

        def _mha(x, ctx, wq, bq, wk, bk, wv, bv, wo, bo, mask):
            B, N, D = x.shape
            M = ctx.shape[1]
            q = _linear(x, wq, bq).reshape(B, N, HEADS, HEAD_DIM).transpose(0, 2, 1, 3)
            k = _linear(ctx, wk, bk).reshape(B, M, HEADS, HEAD_DIM).transpose(0, 2, 1, 3)
            v = _linear(ctx, wv, bv).reshape(B, M, HEADS, HEAD_DIM).transpose(0, 2, 1, 3)
            scores = jnp.einsum('bhqd,bhkd->bhqk', q, k) / np.sqrt(HEAD_DIM).astype(np.float32)
            if mask is not None:
                scores = jnp.where(mask == 0, NEG, scores)
            attn = jax.nn.softmax(scores, axis=-1)
            out = jnp.einsum('bhqk,bhkd->bhqd', attn, v)
            out = out.transpose(0, 2, 1, 3).reshape(B, N, D)
            return _linear(out, wo, bo)

        def _ln(x, g, b):
            mu = jnp.mean(x, axis=-1, keepdims=True)
            var = jnp.mean(jnp.square(x - mu), axis=-1, keepdims=True)
            return (x - mu) * jax.lax.rsqrt(var + EPS) * g + b
        key = jax.random.key(seed)
        ks = jax.random.split(key, 24)
        B, N, M = (2, 1024, 512)
        s = 0.02
        d = {'x': jax.random.normal(ks[0], (B, N, DIM), jnp.float32), 'memory': jax.random.normal(ks[1], (B, M, DIM), jnp.float32), 'mask': jnp.tril(jnp.ones((N, N), jnp.int32))[None, None]}
        i = 2
        for p in ['sa', 'ca']:
            for nm in ['q', 'k', 'v', 'o']:
                d[f'{p}_w{nm}'] = jax.random.normal(ks[i], (DIM, DIM), jnp.float32) * s
                i += 1
                d[f'{p}_b{nm}'] = jnp.zeros((DIM,), jnp.float32)
        d['ff_w1'] = jax.random.normal(ks[i], (4 * DIM, DIM), jnp.float32) * s
        i += 1
        d['ff_b1'] = jnp.zeros((4 * DIM,), jnp.float32)
        d['ff_w2'] = jax.random.normal(ks[i], (DIM, 4 * DIM), jnp.float32) * s
        i += 1
        d['ff_b2'] = jnp.zeros((DIM,), jnp.float32)
        for j in (1, 2, 3):
            d[f'ln{j}_g'] = jnp.ones((DIM,), jnp.float32)
            d[f'ln{j}_b'] = jnp.zeros((DIM,), jnp.float32)
        return d
    _L1_xattn_all = _L1_xattn_setup()
    _L1_xattn_in = {k: v for k, v in _L1_xattn_all.items() if k in ('sa_wq', 'sa_bq', 'sa_wk', 'sa_bk', 'sa_wv', 'sa_bv', 'sa_wo', 'sa_bo', 'ca_wq', 'ca_bq', 'ca_wk', 'ca_bk', 'ca_wv', 'ca_bv', 'ca_wo', 'ca_bo', 'ff_w1', 'ff_b1', 'ff_w2', 'ff_b2', 'ln1_g', 'ln1_b', 'ln2_g', 'ln2_b', 'ln3_g', 'ln3_b')}
    del _L1_xattn_all
    return {'x': x, 'ctx_1024': ctx_1024, 'fside_Bx1xSxS2_0': fside_Bx1xSxS2_0, 'mask_Bx1x1xS2_ik0': mask_Bx1x1xS2_ik0, 'mask_1x1xSxS_ik0': mask_1x1xSxS_ik0, 'L0_xattn_w_q': _L0_xattn_in['w_q'], 'L0_xattn_w_k': _L0_xattn_in['w_k'], 'L0_xattn_w_v': _L0_xattn_in['w_v'], 'L0_xattn_w_o': _L0_xattn_in['w_o'], 'L0_xattn_ln_g': _L0_xattn_in['ln_g'], 'L0_xattn_ln_b': _L0_xattn_in['ln_b'], 'L1_xattn_sa_wq': _L1_xattn_in['sa_wq'], 'L1_xattn_sa_bq': _L1_xattn_in['sa_bq'], 'L1_xattn_sa_wk': _L1_xattn_in['sa_wk'], 'L1_xattn_sa_bk': _L1_xattn_in['sa_bk'], 'L1_xattn_sa_wv': _L1_xattn_in['sa_wv'], 'L1_xattn_sa_bv': _L1_xattn_in['sa_bv'], 'L1_xattn_sa_wo': _L1_xattn_in['sa_wo'], 'L1_xattn_sa_bo': _L1_xattn_in['sa_bo'], 'L1_xattn_ca_wq': _L1_xattn_in['ca_wq'], 'L1_xattn_ca_bq': _L1_xattn_in['ca_bq'], 'L1_xattn_ca_wk': _L1_xattn_in['ca_wk'], 'L1_xattn_ca_bk': _L1_xattn_in['ca_bk'], 'L1_xattn_ca_wv': _L1_xattn_in['ca_wv'], 'L1_xattn_ca_bv': _L1_xattn_in['ca_bv'], 'L1_xattn_ca_wo': _L1_xattn_in['ca_wo'], 'L1_xattn_ca_bo': _L1_xattn_in['ca_bo'], 'L1_xattn_ff_w1': _L1_xattn_in['ff_w1'], 'L1_xattn_ff_b1': _L1_xattn_in['ff_b1'], 'L1_xattn_ff_w2': _L1_xattn_in['ff_w2'], 'L1_xattn_ff_b2': _L1_xattn_in['ff_b2'], 'L1_xattn_ln1_g': _L1_xattn_in['ln1_g'], 'L1_xattn_ln1_b': _L1_xattn_in['ln1_b'], 'L1_xattn_ln2_g': _L1_xattn_in['ln2_g'], 'L1_xattn_ln2_b': _L1_xattn_in['ln2_b'], 'L1_xattn_ln3_g': _L1_xattn_in['ln3_g'], 'L1_xattn_ln3_b': _L1_xattn_in['ln3_b']}

def reference(x, ctx_1024, fside_Bx1xSxS2_0, mask_Bx1x1xS2_ik0, mask_1x1xSxS_ik0, L0_xattn_w_q, L0_xattn_w_k, L0_xattn_w_v, L0_xattn_w_o, L0_xattn_ln_g, L0_xattn_ln_b, L1_xattn_sa_wq, L1_xattn_sa_bq, L1_xattn_sa_wk, L1_xattn_sa_bk, L1_xattn_sa_wv, L1_xattn_sa_bv, L1_xattn_sa_wo, L1_xattn_sa_bo, L1_xattn_ca_wq, L1_xattn_ca_bq, L1_xattn_ca_wk, L1_xattn_ca_bk, L1_xattn_ca_wv, L1_xattn_ca_bv, L1_xattn_ca_wo, L1_xattn_ca_bo, L1_xattn_ff_w1, L1_xattn_ff_b1, L1_xattn_ff_w2, L1_xattn_ff_b2, L1_xattn_ln1_g, L1_xattn_ln1_b, L1_xattn_ln2_g, L1_xattn_ln2_b, L1_xattn_ln3_g, L1_xattn_ln3_b):
    import jax
    import jax.numpy as jnp

    def _L0_xattn_ref(q, k, v, add_attn, mask, w_q, w_k, w_v, w_o, ln_g, ln_b):
        import jax, jax.numpy as jnp
        import numpy as np
        N_HEAD = 16
        D_IN = 512
        D_K = 64
        D_V = 64
        LN_EPS = 1e-06
        NEG_INF = -1000000000.0
        B, L, _ = q.shape
        residual = q
        qh = (q @ w_q).reshape(B, L, N_HEAD, D_K).transpose(0, 2, 1, 3)
        kh = (k @ w_k).reshape(B, L, N_HEAD, D_K).transpose(0, 2, 1, 3)
        vh = (v @ w_v).reshape(B, L, N_HEAD, D_V).transpose(0, 2, 1, 3)
        scale = 1.0 / jnp.sqrt(jnp.asarray(D_K, dtype=qh.dtype))
        attn = jnp.einsum('bhqd,bhkd->bhqk', qh * scale, kh) + add_attn
        attn = jnp.where(mask == 0, jnp.asarray(NEG_INF, attn.dtype), attn)
        attn = jax.nn.softmax(attn, axis=-1)
        out = jnp.einsum('bhqk,bhkd->bhqd', attn, vh)
        out = out.transpose(0, 2, 1, 3).reshape(B, L, N_HEAD * D_V)
        out = out @ w_o + residual
        mu = jnp.mean(out, axis=-1, keepdims=True)
        var = jnp.mean(jnp.square(out - mu), axis=-1, keepdims=True)
        out = (out - mu) / jnp.sqrt(var + LN_EPS) * ln_g + ln_b
        return out

    def _L1_xattn_ref(x, memory, mask, sa_wq, sa_bq, sa_wk, sa_bk, sa_wv, sa_bv, sa_wo, sa_bo, ca_wq, ca_bq, ca_wk, ca_bk, ca_wv, ca_bv, ca_wo, ca_bo, ff_w1, ff_b1, ff_w2, ff_b2, ln1_g, ln1_b, ln2_g, ln2_b, ln3_g, ln3_b):
        import jax, jax.numpy as jnp
        import numpy as np
        DIM = 512
        HEADS = 16
        HEAD_DIM = DIM // HEADS
        NEG = -1e+30
        EPS = 1e-05

        def _linear(x, w, b):
            return jnp.einsum('bnd,od->bno', x, w) + b

        def _mha(x, ctx, wq, bq, wk, bk, wv, bv, wo, bo, mask):
            B, N, D = x.shape
            M = ctx.shape[1]
            q = _linear(x, wq, bq).reshape(B, N, HEADS, HEAD_DIM).transpose(0, 2, 1, 3)
            k = _linear(ctx, wk, bk).reshape(B, M, HEADS, HEAD_DIM).transpose(0, 2, 1, 3)
            v = _linear(ctx, wv, bv).reshape(B, M, HEADS, HEAD_DIM).transpose(0, 2, 1, 3)
            scores = jnp.einsum('bhqd,bhkd->bhqk', q, k) / np.sqrt(HEAD_DIM).astype(np.float32)
            if mask is not None:
                scores = jnp.where(mask == 0, NEG, scores)
            attn = jax.nn.softmax(scores, axis=-1)
            out = jnp.einsum('bhqk,bhkd->bhqd', attn, v)
            out = out.transpose(0, 2, 1, 3).reshape(B, N, D)
            return _linear(out, wo, bo)

        def _ln(x, g, b):
            mu = jnp.mean(x, axis=-1, keepdims=True)
            var = jnp.mean(jnp.square(x - mu), axis=-1, keepdims=True)
            return (x - mu) * jax.lax.rsqrt(var + EPS) * g + b
        x = _ln(x + _mha(x, x, sa_wq, sa_bq, sa_wk, sa_bk, sa_wv, sa_bv, sa_wo, sa_bo, mask), ln1_g, ln1_b)
        x = _ln(x + _mha(x, memory, ca_wq, ca_bq, ca_wk, ca_bk, ca_wv, ca_bv, ca_wo, ca_bo, None), ln2_g, ln2_b)
        h = jax.nn.relu(_linear(x, ff_w1, ff_b1))
        x = _ln(x + _linear(h, ff_w2, ff_b2), ln3_g, ln3_b)
        return x
    x = _L0_xattn_ref(x, ctx_1024, ctx_1024, fside_Bx1xSxS2_0, mask_Bx1x1xS2_ik0, L0_xattn_w_q, L0_xattn_w_k, L0_xattn_w_v, L0_xattn_w_o, L0_xattn_ln_g, L0_xattn_ln_b)
    x = _L1_xattn_ref(x, ctx_1024, mask_1x1xSxS_ik0, L1_xattn_sa_wq, L1_xattn_sa_bq, L1_xattn_sa_wk, L1_xattn_sa_bk, L1_xattn_sa_wv, L1_xattn_sa_bv, L1_xattn_sa_wo, L1_xattn_sa_bo, L1_xattn_ca_wq, L1_xattn_ca_bq, L1_xattn_ca_wk, L1_xattn_ca_bk, L1_xattn_ca_wv, L1_xattn_ca_bv, L1_xattn_ca_wo, L1_xattn_ca_bo, L1_xattn_ff_w1, L1_xattn_ff_b1, L1_xattn_ff_w2, L1_xattn_ff_b2, L1_xattn_ln1_g, L1_xattn_ln1_b, L1_xattn_ln2_g, L1_xattn_ln2_b, L1_xattn_ln3_g, L1_xattn_ln3_b)
    return x

_drawn_inputs = setup_inputs


def setup_inputs(seed=0):
    import zlib

    import numpy as np

    out = dict(_drawn_inputs(seed))
    spreads = {'L0_xattn_ln_g': (1.0, 0.2),
     'L0_xattn_ln_b': (0.0, 0.1),
     'L1_xattn_sa_bq': (0.0, 0.8),
     'L1_xattn_sa_bk': (0.0, 0.8),
     'L1_xattn_sa_bv': (0.0, 0.1),
     'L1_xattn_sa_bo': (0.0, 0.1),
     'L1_xattn_ca_bq': (0.0, 0.8),
     'L1_xattn_ca_bk': (0.0, 0.8),
     'L1_xattn_ca_bv': (0.0, 0.1),
     'L1_xattn_ca_bo': (0.0, 0.1),
     'L1_xattn_ff_b1': (0.0, 0.1),
     'L1_xattn_ff_b2': (0.0, 0.1),
     'L1_xattn_ln1_g': (1.0, 0.2),
     'L1_xattn_ln1_b': (0.0, 0.1),
     'L1_xattn_ln2_g': (1.0, 0.2),
     'L1_xattn_ln2_b': (0.0, 0.1),
     'L1_xattn_ln3_g': (1.0, 0.2),
     'L1_xattn_ln3_b': (0.0, 0.1)}
    factors = {'L1_xattn_sa_wq': 8.0,
     'L1_xattn_sa_wk': 8.0,
     'L1_xattn_ca_wq': 7.865,
     'L1_xattn_ca_wk': 7.731}
    for name, (base, spread) in spreads.items():
        noise = np.random.default_rng([zlib.crc32(name.encode()), seed]).standard_normal(out[name].shape)
        drawn = base * np.exp(spread * noise) if base else spread * noise
        out[name] = jnp.asarray(drawn.astype(out[name].dtype))
    for name, factor in factors.items():
        out[name] = (out[name] * factor).astype(out[name].dtype)
    return out
```

```python
from contextlib import ExitStack, contextmanager

B, S, D, FF = 8, 512, 512, 2048
P = 128
NT = S // P
KT = D // P
NF = FF // P
AD = 512
NG = AD // P
LAG = 3

COL = {"SA": 0, "CA": 12, "FF": 24, "ZERO": 40}
NCOL = 40
CONSTS = 4
ROW = {"L0": 0, "SA": 1, "CA": 2, "FF": 3}


class Stage:

    def __init__(self, name, dk, block, src, res, dst, context, bias, norm, eps, rows, cols):
        self.name, self.dk, self.block = name, dk, block
        self.src, self.res, self.dst = src, res, dst
        self.context, self.bias, self.norm, self.eps = context, bias, norm, eps
        self.rows, self.cols = rows, cols
        self.heads = AD // dk
        self.per_group = P // dk
        self.steps = self.heads * NT
        self.scale = float(dk) ** -0.5


STAGES = [
    Stage("L0a", 64, 0, "x", "x", "half", True, "side", False, 0.0, None, "ZERO"),
    Stage("L0b", 64, 4, "x", "half", "x1", True, "side", True, 1e-6, "L0", "ZERO"),
    Stage("SA", 32, 8, "x1", "x1", "x2", False, "mask", True, 1e-5, "SA", "SA"),
    Stage("CA", 32, 12, "x2", "x2", "x3", True, None, True, 1e-5, "CA", "CA"),
]
FF_BLOCK, FF_EPS = 16, 1e-5


def schedule(st, prev, nxt):
    T = st.steps
    span = T // NG
    jobs = [[] for _ in range(T)]
    for tt in range(NT):
        jobs[3 + tt].append(("V", tt))
        if prev:
            jobs[6 + tt].append(("RES", tt))
            jobs[7 + tt].append(("OUT", tt))
            jobs[8 + tt].append(("NORM", tt))
    for g in range(NG):
        at = g * span
        if g + 1 < NG:
            jobs[at + span // 4].append(("Q", g + 1))
            jobs[at + span // 2].append(("K", g + 1))
        elif nxt:
            jobs[at + span // 2].append(("Q", 0))
            jobs[at + 3 * span // 4].append(("K", 0))
    slots = []
    for s in range(T):
        ev = []
        if st.bias == "side" and s < NT:
            ev.append(("SIDE", s))
        if nxt and 0 <= s - (NG - 1) * span < NT:
            ev.append(("X", s - (NG - 1) * span))
            if st.context:
                ev.append(("C", s - (NG - 1) * span))
        ev.append(("SCORE", s))
        if s >= 1:
            ev.append(("RECIP", s - 1))
        elif prev:
            ev.append(("RECIP", T - 1))
        if s >= LAG:
            ev.append(("TURN", s - LAG))
        elif prev:
            ev.append(("TURN", T + s - LAG))
        h, r = divmod(s - LAG - 1, NT)
        if r == NT - 1 and (h >= 0 or prev):
            ev.append(("PV", h % st.heads))
        ev += jobs[s]
        if st.bias == "side" and nxt and s == T - 1:
            ev.append(("ROWMASK", 0))
        slots.append(ev)
    return slots


def prologue(st):
    ev = []
    for tt in range(NT):
        ev += [("X", tt)] + ([("C", tt)] if st.context else [])
    ev += [("Q", 0), ("K", 0)]
    if st.bias == "side":
        ev.append(("ROWMASK", 0))
    return ev


def drain(st):
    T = st.steps
    ev = [("RECIP", T - 1)] + [("TURN", t) for t in range(T - LAG, T)] + [("PV", st.heads - 1)]
    ev += [("RES", tt) for tt in range(NT)]
    for tt in range(NT):
        ev.append(("OUT", tt))
        ev.append(("NORM", tt))
    return ev


class Tally:

    def __init__(self, sem, unit=1, credit=0):
        self.sem, self.unit, self.credit = sem, unit, credit
        self.n, self.per, self.turn = 0, 0, None

    def next(self):
        self.n += 1
        return self.n - 1

    def done(self, n):
        v = self.unit * (n + 1) + self.credit
        return v if self.turn is None else self.turn * (self.per * self.unit) + v


class RingTally(Tally):

    def __init__(self, sems, credit=0):
        Tally.__init__(self, None, 16, credit)
        self.sems = sems

    def slot(self, n):
        return n % len(self.sems)

    def sem_of(self, n):
        return self.sems[n % len(self.sems)]

    def done(self, n):
        R = len(self.sems)
        v = 16 * (n // R + 1) + self.credit
        return v if self.turn is None else self.turn * (self.per // R * 16) + v


@contextmanager
def turns(eng, count, tallies):
    first = [t.n for t, _ in tallies]
    with eng.Fori(0, count) as r:
        for t, per in tallies:
            t.per, t.turn = per, r
        yield r
    for (t, per), n in zip(tallies, first):
        assert t.n - n == per, (t.sem, t.n - n, per)
        t.turn = None
        t.n += per * (count - 1)


def build(nc, x, ctx_t, side, key_mask, pair_mask, w, rows, cols, out):
    import concourse.bass as bass
    from concourse import mybir

    F32, F32R, I32 = mybir.dt.float32, mybir.dt.float32r, mybir.dt.int32
    ALU, ACT = mybir.AluOpType, mybir.ActivationFunctionType
    BIG = 3.0e38
    FILL = 1.0e30

    dram = {"x": x, "out": out}
    for name in ("half", "x1", "x2", "x3"):
        dram[name] = nc.dram_tensor(name, (B, S, D), F32, kind="Internal").ap()

    with ExitStack() as stack:
        def sb(name, shape, dt=F32):
            return stack.enter_context(nc.sbuf_tensor(name, shape, dt))

        def sem(name):
            return stack.enter_context(nc.semaphore(name))

        W = sb("W", [P, 8, KT, D], F32R)
        R = sb("R", [P, 8, KT, D], F32R)
        cT = R[:, 0:2]
        VAL = R[:, 2:4].rearrange("p a k n -> p (a k n)").rearrange("p (k n) -> p k n", k=NT)
        PT = [R[:, 4 + 2 * i:6 + 2 * i] for i in range(2)]
        xT = sb("xT", [P, 2, KT, S], F32R)
        xs = sb("xs", [P, 2, D])
        cs = sb("cs", [P, 2, S])
        QK = sb("QK", [P, 2, 2, 2, S], F32R)
        PR = sb("PR", [P, 4, S])
        FB = sb("FB", [P, NT, S])
        OT = sb("OT", [P, 2, NG, S], F32R)
        OG = sb("OG", [P, S])
        Y = sb("Y", [P, NT, D])
        ROWS = sb("ROWS", [P, 4, D])
        COLS = sb("COLS", [P, NCOL + NG])
        MN = sb("MN", [P, 64])
        SM = sb("SM", [P, 64])
        RS = sb("RS", [P, 64])
        ID = sb("ID", [P, P])
        ST = sb("ST", [P, 6])
        MV = sb("MV", [P, NT, 2])
        VE = sb("VE", [P, NT])
        RD = sb("RD", [P, NT])
        CONST = sb("CONST", [P, 3])
        EPS = {1e-6: 1, 1e-5: 2}
        HF = PR
        HH = [QK[:, i, 0, 0] for i in range(2)]
        HL = [QK[:, i, 0, 1] for i in range(2)]

        psS = stack.enter_context(nc.psum_tensor("psS", [P, 2, 512], F32))
        psT = stack.enter_context(nc.psum_tensor("psT", [P, 2, 512], F32))
        psJ = stack.enter_context(nc.psum_tensor("psJ", [P, 2, 512], F32))
        psV = stack.enter_context(nc.psum_tensor("psV", [P, 2, 512], F32))

        xs_full = [sem(f"xs_full{i}") for i in range(2)]
        cs_full = [sem(f"cs_full{i}") for i in range(2)]
        side_full = [sem(f"side_full{i}") for i in range(NT)]
        mask_full = sem("mask_full")
        rows_full = sem("rows_full")
        y_full = [sem(f"y_full{i}") for i in range(NT)]
        y_stored = [sem(f"y_stored{i}") for i in range(NT)]
        const_ready = sem("const_ready")
        ident_ready = sem("ident_ready")
        ident_zero = sem("ident_zero")
        x_hi = sem("x_hi")
        cs_hi = sem("cs_hi")
        cs_lo = sem("cs_lo")
        s_full = sem("s_full")
        s_evac = sem("s_evac")
        exp_done = sem("exp_done")
        recip_done = sem("recip_done")
        p_ready = sem("p_ready")
        t_full = sem("t_full")
        t_hi = sem("t_hi")
        t_evac = sem("t_evac")
        pv_full = sem("pv_full")
        pv_half = sem("pv_half")
        pv_evac = sem("pv_evac")
        o_hi = sem("o_hi")
        o_lo = sem("o_lo")
        j_full = sem("j_full")
        j_hi = sem("j_hi")
        j_evac = sem("j_evac")
        mask_ready = sem("mask_ready")
        side_ready = sem("side_ready")
        side_half = sem("side_half")
        res_ready = sem("res_ready")
        mv_ready = sem("mv_ready")
        var_eps = sem("var_eps")
        rstd = sem("rstd")
        y_norm = sem("y_norm")
        y_gain = sem("y_gain")
        y_done = sem("y_done")
        y_sum = sem("y_sum")
        conv_done = sem("conv_done")
        u_full = sem("u_full")
        h_full = sem("h_full")
        h_hi = sem("h_hi")
        h_lo = sem("h_lo")
        h_used = sem("h_used")
        acc_evac = sem("acc_evac")
        gate_dve = sem("gate_dve")
        gate_pool = sem("gate_pool")

        def w_part(b, part):
            return (W if b < 4 else R)[:, 2 * (b % 4) + part]

        def f32(ap):
            return ap.bitcast(F32)

        def counts(st):
            T = st.steps
            return dict(xs=NT, x_hi=NT, cs=KT, cs_hi=KT, cs_lo=KT, s=T, exp=T, recip=T, p=T, t=T + NT, t_hi=T,
                        pv=st.heads, pv_half=st.heads, o_hi=NG, o_lo=NG, j=2 * NG + 2 * NT, j_hi=2 * NG + NT,
                        mask=1, mask_ready=1, side=NT, side_ready=NT, res=NT, y=NT, mv=NT, var=NT, rstd=NT, y_norm=NT,
                        gain=NT, y_done=NT, y_sum=2 * NT)

        def loop(eng, count, tal, per):
            return turns(eng, count, [(tal[k], per[k]) for k in tal if k in per])

        block = stack.enter_context(nc.Block())

        @block.sync
        def _(sp):
            tal = dict(xs=RingTally(xs_full), x_hi=Tally(x_hi, credit=2), cs=RingTally(cs_full),
                       cs_lo=Tally(cs_lo, credit=2), s=Tally(s_evac, credit=2), side=RingTally(side_full),
                       side_ready=Tally(side_ready), y=RingTally(y_stored, credit=16), y_norm=Tally(y_norm),
                       y_done=Tally(y_done))
            for tt in range(NT):
                sp.sem_inc(y_stored[tt], 16)
            sp.dma_start(COLS[:, 0:NCOL], cols).then_inc(rows_full, 16)

            def load_x(src, b, tt):
                n = tal["x_hi"].next()
                sp.wait_ge(x_hi, tal["x_hi"].done(n - 2))
                i = tal["xs"].next()
                sp.dma_start(xs[:, tal["xs"].slot(i)], dram[src][b, tt * P:(tt + 1) * P, :]).then_inc(
                    tal["xs"].sem_of(i), 16)

            def load_c(src):
                n = tal["cs_lo"].next()
                sp.wait_ge(cs_lo, tal["cs_lo"].done(n - 2))
                i = tal["cs"].next()
                sp.dma_start(cs[:, tal["cs"].slot(i)], src).then_inc(tal["cs"].sem_of(i), 16)

            def load_side(b, qt):
                i = tal["side"].next()
                sp.dma_start(FB[:, qt], side[b, 0, qt * P:(qt + 1) * P, :]).then_inc(tal["side"].sem_of(i), 16)

            def load_mask(b):
                sp.dma_start(ROWS[:, 0].bitcast(I32), key_mask[b, 0, 0:1, :].to_broadcast([P, S])).then_inc(mask_full, 16)

            def load_res(st_res, b, tt):
                i = tal["y"].next()
                sp.wait_ge(y_stored[tt], tal["y"].done(i - NT))
                sp.dma_start(Y[:, tt], dram[st_res][b, tt * P:(tt + 1) * P, :]).then_inc(y_full[tt], 16)

            def store(name, norm, b, tt):
                which, ready = ("y_done", y_done) if norm else ("y_norm", y_norm)
                tal["y_norm" if norm else "y_done"].next() if False else None
                n = tal[which].next()
                sp.wait_ge(ready, tal[which].done(n))
                sp.dma_start(dram[name][b, tt * P:(tt + 1) * P, :], Y[:, tt]).then_inc(y_stored[tt], 16)

            def begin(rows, bias_row, blocks):
                if tal["y"].n:
                    for tt in range(NT):
                        sp.wait_ge(y_stored[tt], tal["y"].done(tal["y"].n - NT + tt))
                if rows is not None:
                    for k in range(0 if bias_row else 1, 3):
                        sp.dma_start(ROWS[:, k + 1 if k else 0], rows_d(rows, k)).then_inc(rows_full, 16)
                for b in blocks:
                    for kt in range(KT):
                        load_c(w[b, kt * P:(kt + 1) * P, :])

            def rows_d(name, k):
                return rows[ROW[name], k:k + 1, :].to_broadcast([P, D])

            for st in STAGES:
                T, per = st.steps, counts(st)
                begin(st.rows, st.cols != "ZERO", range(st.block, st.block + 4))

                def inputs(b, first):
                    for tt in range(NT):
                        load_x(st.src, b, tt)
                        if st.context:
                            load_c(ctx_t[b, tt * P:(tt + 1) * P, :])
                    if st.bias == "side":
                        if not first:
                            sp.wait_ge(side_ready, tal["side_ready"].done(tal["side_ready"].n - 1))
                        load_mask(b)
                        for qt in range(NT):
                            if not first:
                                sp.wait_ge(s_evac, tal["s"].done(tal["s"].n - NT + qt))
                            load_side(b, qt)

                def body(b, prev, nxt):
                    if prev is not None:
                        outputs(prev)
                    tal["s"].n += T
                    tal["side_ready"].n += NT
                    if nxt is not None:
                        inputs(nxt, False)

                def outputs(b):
                    for tt in range(NT):
                        load_res(st.res, b, tt)
                    for tt in range(NT):
                        store(st.dst, st.norm, b, tt)

                if st.bias == "mask":
                    for qt in range(NT):
                        i = tal["side"].next()
                        sp.dma_start(FB[:, qt].bitcast(I32), pair_mask[0, 0, qt * P:(qt + 1) * P, :]).then_inc(
                            tal["side"].sem_of(i), 16)
                inputs(0, True)
                body(0, None, 1)
                keep = ["xs", "x_hi", "s", "side_ready", "y"] + (["cs", "cs_lo"] if st.context else [])
                keep += ["side"] if st.bias == "side" else []
                keep += ["y_done"] if st.norm else ["y_norm"]
                with loop(sp, B - 2, {k: tal[k] for k in keep}, per) as r:
                    body(r + 1, r, r + 2)
                body(B - 1, B - 2, None)
                outputs(B - 1)
                if st.norm:
                    tal["y_norm"].n += B * NT
                if st.bias != "side":
                    tal["side_ready"].n -= B * NT

            begin("FF", True, range(FF_BLOCK, FF_BLOCK + 8))

            def ff_inputs(b):
                for tt in range(NT):
                    load_x("x3", b, tt)

            def ff_residuals(b):
                for tt in range(NT):
                    load_res("x3", b, tt)

            def ff_stores(b):
                for tt in range(NT):
                    store("out", True, b, tt)

            ff_inputs(0)
            with loop(sp, B - 1, {k: tal[k] for k in ("xs", "x_hi", "y", "y_done")},
                      dict(xs=NT, x_hi=NT, y=NT, y_done=NT)) as r:
                ff_residuals(r)
                ff_inputs(r + 1)
                ff_stores(r)
            ff_residuals(B - 1)
            ff_stores(B - 1)
            for tt in range(NT):
                sp.wait_ge(y_stored[tt], tal["y"].done(tal["y"].n - NT + tt))

        @block.tensor
        def _(pe):
            tal = dict(xs=RingTally(xs_full), cs_lo=Tally(cs_lo, credit=2), s=Tally(s_evac, credit=2),
                       p=Tally(p_ready), t=Tally(t_evac, credit=2), pv=Tally(pv_evac, credit=2),
                       o_lo=Tally(o_lo, credit=1), j=Tally(j_evac, credit=2))
            pe.sem_inc(h_used, 2)
            pe.wait_ge(ident_ready, 1)

            def three(dst, a, b, first=True, last=True):
                nc.tensor.matmul(dst, a[0], b[0], start=first, stop=False)
                nc.tensor.matmul(dst, a[0], b[1], start=False, stop=False)
                return nc.tensor.matmul(dst, a[1], b[0], start=False, stop=last)

            def parts(t, kt, cols):
                return [t[:, p, kt, cols] for p in range(2)]

            def w_parts(b, kt, cols):
                return [w_part(b, p)[:, kt, cols] for p in range(2)]

            def x_turn(tt):
                i = tal["xs"].next()
                n = tal["t"].next()
                pe.wait_ge(tal["xs"].sem_of(i), tal["xs"].done(i))
                pe.wait_ge(t_evac, tal["t"].done(n - 2))
                for kt in range(KT):
                    mm = nc.tensor.transpose(psT[:, n % 2, kt * P:(kt + 1) * P],
                                             xs[:, tal["xs"].slot(i), kt * P:(kt + 1) * P], ID[:, :])
                mm.then_inc(t_full, 1)
                return n

            def weights(count):
                for _ in range(count):
                    n = tal["cs_lo"].next()
                pe.wait_ge(cs_lo, tal["cs_lo"].done(n))

            for st in STAGES:
                T, per, dk = st.steps, counts(st), st.dk
                memo = {}
                src = cT if st.context else xT
                weights(4 * KT)

                def run(events):
                    for kind, k in events:
                        if kind == "X":
                            memo["x"] = x_turn(k)
                        elif kind == "C":
                            memo["c"] = tal["cs_lo"].next()
                        elif kind in ("Q", "K"):
                            if k == 0 and kind == "Q":
                                pe.wait_ge(t_evac, tal["t"].done(memo["x"]))
                            if k == 0 and kind == "K" and st.context:
                                pe.wait_ge(cs_lo, tal["cs_lo"].done(memo["c"]))
                            n = tal["j"].next()
                            pe.wait_ge(j_evac, tal["j"].done(n - 2))
                            data, b = (xT, 0) if kind == "Q" else (src, 1)
                            for kt in range(KT):
                                mm = three(psJ[:, n % 2], w_parts(b, kt, slice(k * P, (k + 1) * P)),
                                           parts(data, kt, slice(0, S)), kt == 0, kt == KT - 1)
                            mm.then_inc(j_full, 1)
                            memo["k", k] = n
                        elif kind == "SCORE":
                            h, qt = divmod(k, NT)
                            g, j = divmod(h, st.per_group)
                            n = tal["s"].next()
                            if j == 0 and qt == 0:
                                last = memo["k", g] if g else tal["j"].n - 1
                                pe.wait_ge(j_evac, tal["j"].done(last))
                            pe.wait_ge(s_evac, tal["s"].done(n - 2))
                            dims = slice(j * dk, (j + 1) * dk)
                            q = [QK[dims, g % 2, 0, p, qt * P:(qt + 1) * P] for p in range(2)]
                            kk = [QK[dims, g % 2, 1, p, :] for p in range(2)]
                            three(psS[:, n % 2], q, kk).then_inc(s_full, 1)
                        elif kind == "TURN":
                            n = tal["t"].next()
                            i = tal["p"].next()
                            pe.wait_ge(p_ready, tal["p"].done(i))
                            pe.wait_ge(t_evac, tal["t"].done(n - 2))
                            for kt in range(NT):
                                mm = nc.tensor.transpose(psT[:, n % 2, kt * P:(kt + 1) * P],
                                                         PR[:, k % 4, kt * P:(kt + 1) * P], ID[:, :])
                            mm.then_inc(t_full, 1)
                            memo["t"] = n
                        elif kind == "PV":
                            n = tal["pv"].next()
                            pe.wait_ge(t_evac, tal["t"].done(memo["t"]))
                            pe.wait_ge(pv_evac, tal["pv"].done(n - 2))
                            if k == 0:
                                pe.wait_ge(j_evac, tal["j"].done(memo["v"]))
                            for kt in range(NT):
                                for p in range(2):
                                    mm = nc.tensor.matmul(psV[0:2 * dk, n % 2], VAL[:, kt, 2 * dk * k:2 * dk * (k + 1)],
                                                          PT[k % 2][:, p, kt, :], start=(kt == 0 and p == 0),
                                                          stop=(kt == NT - 1 and p == 1))
                            mm.then_inc(pv_full, 1)
                        elif kind == "V":
                            n = tal["j"].next()
                            pe.wait_ge(j_evac, tal["j"].done(n - 2))
                            for kt in range(KT):
                                mm = three(psJ[:, n % 2], parts(src, kt, slice(k * P, (k + 1) * P)),
                                           w_parts(2, kt, slice(0, AD)), kt == 0, kt == KT - 1)
                            mm.then_inc(j_full, 1)
                            memo["v"] = n
                        elif kind == "OUT":
                            n = tal["j"].next()
                            if k == 0:
                                for g in range(NG):
                                    i = tal["o_lo"].next()
                                pe.wait_ge(o_lo, tal["o_lo"].done(i))
                            pe.wait_ge(j_evac, tal["j"].done(n - 2))
                            for g in range(NG):
                                mm = three(psJ[:, n % 2], parts(OT, g, slice(k * P, (k + 1) * P)),
                                           w_parts(3, g, slice(0, D)), g == 0, g == NG - 1)
                            mm.then_inc(j_full, 1)

                def body(prev, nxt):
                    for events in schedule(st, prev, nxt):
                        run(events)

                run(prologue(st))
                body(False, True)
                keep = ["xs", "s", "p", "t", "pv", "o_lo", "j"] + (["cs_lo"] if st.context else [])
                with loop(pe, B - 2, {k: tal[k] for k in keep}, per):
                    body(True, True)
                body(True, False)
                run(drain(st))

            tal.update(u=Tally(h_full, credit=2), h=Tally(h_lo, credit=2), acc=Tally(acc_evac, credit=NT))
            weights(8 * KT)
            acc = [psJ[:, 0], psJ[:, 1], psV[:, 0], psV[:, 1]]

            def up(f, x_last):
                n = tal["u"].next()
                if f == 0:
                    pe.wait_ge(t_evac, tal["t"].done(x_last))
                pe.wait_ge(h_full, tal["u"].done(n - 2))
                for kt in range(KT):
                    mm = three(psS[:, n % 2], w_parts(f // 4, kt, slice((f % 4) * P, (f % 4 + 1) * P)),
                               parts(xT, kt, slice(0, S)), kt == 0, kt == KT - 1)
                mm.then_inc(u_full, 1)

            def down(f):
                n = tal["h"].next()
                pe.wait_ge(h_lo, tal["h"].done(n))
                if f == 0:
                    for tt in range(NT):
                        i = tal["acc"].next()
                    pe.wait_ge(acc_evac, tal["acc"].done(i - NT))
                for tt in range(NT):
                    h = [t[n % 2][:, tt * P:(tt + 1) * P] for t in (HH, HL)]
                    mm = three(acc[tt], h, w_parts(4 + f // 4, f % 4, slice(0, D)), f == 0, f == NF - 1)
                mm.then_inc(h_used, 1)

            def ff(x_last, nxt):
                up(0, x_last)
                for f in range(1, NF):
                    up(f, None)
                    down(f - 1)
                if nxt:
                    for tt in range(NT):
                        x_turn(tt)
                down(NF - 1)

            for tt in range(NT):
                x_turn(tt)
            with loop(pe, B - 1, {k: tal[k] for k in ("xs", "t", "u", "h", "acc")},
                      dict(xs=NT, t=NT, u=NF, h=NF, acc=NT)):
                ff(tal["t"].n - 1, True)
            ff(tal["t"].n - 1, False)

        @block.scalar
        def _(act):
            tal = dict(cs=RingTally(cs_full), t=Tally(t_full), s=Tally(s_evac, credit=2), pv=Tally(pv_full),
                       o_lo=Tally(o_lo, credit=1), g=Tally(pv_evac, credit=2), j=Tally(j_full))
            act.sem_inc(x_hi, 2)
            act.sem_inc(h_full, 2)
            act.wait_ge(const_ready, CONSTS)
            act.wait_ge(rows_full, 16)

            def split_hi(dst):
                i = tal["cs"].next()
                act.wait_ge(tal["cs"].sem_of(i), tal["cs"].done(i))
                nc.scalar.activation(dst, cs[:, tal["cs"].slot(i)], ACT.Copy).then_inc(cs_hi, 1)

            def x_hi_part(tt):
                n = tal["t"].next()
                act.wait_ge(t_full, tal["t"].done(n))
                nc.scalar.activation(xT[:, 0, :, tt * P:(tt + 1) * P],
                                     psT[:, n % 2].rearrange("p (k t) -> p k t", k=KT), ACT.Copy).then_inc(x_hi, 1)

            for st in STAGES:
                T, per, dk = st.steps, counts(st), st.dk
                for b in range(4):
                    for kt in range(KT):
                        split_hi(w_part(b, 0)[:, kt])

                def run(events):
                    for kind, k in events:
                        if kind == "X":
                            x_hi_part(k)
                        elif kind == "C":
                            split_hi(cT[:, 0, k])
                        elif kind in ("Q", "K"):
                            n = tal["j"].next()
                            qk = "QK".index(kind)
                            col = COL[st.cols] + (0 if st.cols == "ZERO" else qk * NG) + k
                            act.wait_ge(j_full, tal["j"].done(n))
                            nc.scalar.activation(QK[:, k % 2, qk, 0], psJ[:, n % 2], ACT.Identity,
                                                 bias=COLS[:, col:col + 1]).then_inc(j_hi, 1)
                        elif kind == "SCORE":
                            n = tal["s"].next()
                            act.wait_ge(s_evac, tal["s"].done(n))
                            nc.scalar.activation(PR[:, k % 4], PR[:, k % 4], ACT.Exp, bias=MN[:, k:k + 1], scale=-1.0,
                                                 accum_out=SM[:, k:k + 1]).then_inc(exp_done, 1)
                        elif kind == "TURN":
                            h, qt = divmod(k, NT)
                            n = tal["t"].next()
                            act.wait_ge(t_full, tal["t"].done(n))
                            nc.scalar.activation(PT[h % 2][:, 0, :, qt * P:(qt + 1) * P],
                                                 psT[:, n % 2].rearrange("p (k t) -> p k t", k=NT), ACT.Copy).then_inc(t_hi, 1)
                        elif kind == "PV":
                            g, j = divmod(k, st.per_group)
                            n = tal["pv"].next()
                            act.wait_ge(pv_full, tal["pv"].done(n))
                            if j == 0:
                                i = tal["o_lo"].next()
                                act.wait_ge(o_lo, tal["o_lo"].done(i - 1))
                            nc.scalar.activation(OG[j * dk:(j + 1) * dk, :], psV[dk:2 * dk, n % 2], ACT.Copy).then_inc(pv_half, 1)
                            m = tal["g"].next()
                            if j == st.per_group - 1:
                                col = COL[st.cols] + (0 if st.cols == "ZERO" else 2 * NG) + g
                                act.wait_ge(pv_evac, tal["g"].done(m))
                                nc.scalar.activation(OT[:, 0, g], OG[:, :], ACT.Identity,
                                                     bias=COLS[:, col:col + 1]).then_inc(o_hi, 1)
                        elif kind == "V":
                            n = tal["j"].next()
                            act.wait_ge(j_full, tal["j"].done(n))
                            nc.scalar.activation(VAL[:, k].rearrange("p (h c) -> p h c", c=2 * dk)[:, :, 0:dk],
                                                 psJ[:, n % 2].rearrange("p (h c) -> p h c", c=dk), ACT.Copy).then_inc(j_hi, 1)
                        elif kind == "OUT":
                            tal["j"].next()

                def body(prev, nxt):
                    for events in schedule(st, prev, nxt):
                        run(events)

                run(prologue(st))
                body(False, True)
                keep = ["t", "s", "pv", "o_lo", "g", "j"] + (["cs"] if st.context else [])
                with loop(act, B - 2, {k: tal[k] for k in keep}, dict(per, g=st.heads)):
                    body(True, True)
                body(True, False)
                run(drain(st))

            tal.update(u=Tally(u_full), h=Tally(h_lo, credit=2))
            for b in range(8):
                for kt in range(KT):
                    split_hi(w_part(b, 0)[:, kt])

            def relu(f):
                n = tal["u"].next()
                i = tal["h"].next()
                act.wait_ge(u_full, tal["u"].done(n))
                act.wait_ge(h_lo, tal["h"].done(i - 2))
                nc.scalar.activation(HF[:, n % 2], psS[:, n % 2], ACT.Relu,
                                     bias=COLS[:, COL["FF"] + f:COL["FF"] + f + 1]).then_inc(h_full, 1)

            for tt in range(NT):
                x_hi_part(tt)
            with loop(act, B - 1, {k: tal[k] for k in ("t", "u", "h")}, dict(t=NT, u=NF, h=NF)):
                for f in range(NF):
                    relu(f)
                for tt in range(NT):
                    x_hi_part(tt)
            for f in range(NF):
                relu(f)

        @block.vector
        def _(dve):
            tal = dict(x_hi=Tally(x_hi, credit=2), s=Tally(s_full), exp=Tally(exp_done), t_hi=Tally(t_hi),
                       t=Tally(t_full), pv_half=Tally(pv_half), o_hi=Tally(o_hi), j=Tally(j_full), j_hi=Tally(j_hi),
                       mask=Tally(mask_full, unit=16), side_ready=Tally(side_ready), y=RingTally(y_full),
                       res=Tally(res_ready), rstd=Tally(rstd), y_sum=Tally(y_sum), mask_ready=Tally(mask_ready))
            nc.vector.memset(CONST[:, 0:1], -0.5).then_inc(const_ready, 1)
            nc.vector.memset(CONST[:, 1:2], 1e-6).then_inc(const_ready, 1)
            nc.vector.memset(CONST[:, 2:3], 1e-5).then_inc(const_ready, 1)
            nc.vector.memset(COLS[:, NCOL:NCOL + NG], 0.0).then_inc(const_ready, 1)
            dve.sem_inc(s_evac, 2)
            dve.sem_inc(t_evac, 2)
            dve.sem_inc(pv_evac, 2)
            dve.sem_inc(j_evac, 2)
            dve.sem_inc(o_lo, 1)
            dve.sem_inc(acc_evac, NT)

            def gate():
                dve.sem_inc(gate_dve, 1)

            def x_lo_part(tt):
                n = tal["t"].next()
                i = tal["x_hi"].next()
                dve.wait_ge(x_hi, tal["x_hi"].done(i))
                hi, lo = (xT[:, p, :, tt * P:(tt + 1) * P] for p in range(2))
                nc.vector.tensor_tensor(lo, psT[:, n % 2].rearrange("p (k t) -> p k t", k=KT), f32(hi),
                                        ALU.subtract).then_inc(t_evac, 1)

            def take(tt, psum, norm, bias_row):
                i = tal["y"].next()
                if bias_row:
                    n = tal["res"].next()
                    dve.wait_ge(res_ready, tal["res"].done(n))
                else:
                    dve.wait_ge(y_full[tt], tal["y"].done(i))
                nc.vector.tensor_tensor(Y[:, tt], psum, Y[:, tt], ALU.add).then_inc(
                    *((acc_evac, 1) if psum_is_acc else (j_evac, 1)))

            psum_is_acc = False

            def stats(tt, wait_sem, wait_value):
                dve.wait_ge(wait_sem, wait_value)
                n = tal["y_sum"].next()
                nc.vector.bn_stats(ST[:, :], Y[:, tt]).then_inc(y_sum, 1)
                dve.wait_ge(y_sum, tal["y_sum"].done(n))
                gate()
                nc.vector.bn_aggr(MV[:, tt], ST[:, :]).then_inc(mv_ready, 1)

            def normalise(tt):
                n = tal["rstd"].next()
                dve.wait_ge(rstd, tal["rstd"].done(n))
                nc.vector.tensor_scalar(Y[:, tt], Y[:, tt], MV[:, tt, 0:1], RD[:, tt:tt + 1], ALU.subtract,
                                        ALU.mult).then_inc(y_norm, 1)

            tal["j_own"] = Tally(j_evac, credit=2)
            tal["acc_own"] = Tally(acc_evac, credit=NT)

            for st in STAGES:
                T, per, dk = st.steps, counts(st), st.dk
                if st.bias == "mask":
                    for qt in range(NT):
                        dve.wait_ge(side_full[qt], 16 * (2 * B + 1))
                        nc.vector.tensor_scalar(FB[:, qt], FB[:, qt].bitcast(I32), 0.0, -FILL, ALU.is_equal,
                                                ALU.mult).then_inc(conv_done, 1)

                def run(events):
                    for kind, k in events:
                        if kind == "X":
                            x_lo_part(k)
                        elif kind in ("Q", "K"):
                            n = tal["j"].next()
                            tal["j_own"].next()
                            qk = "QK".index(kind)
                            col = COL[st.cols] + (0 if st.cols == "ZERO" else qk * NG) + k
                            i = tal["j_hi"].next()
                            dve.wait_ge(j_hi, tal["j_hi"].done(i))
                            nc.vector.scalar_tensor_tensor(
                                out=QK[:, k % 2, qk, 1], in0=psJ[:, n % 2], scalar=COLS[:, col:col + 1],
                                in1=f32(QK[:, k % 2, qk, 0]), op0=ALU.add, op1=ALU.subtract).then_inc(j_evac, 1)
                        elif kind == "ROWMASK":
                            i = tal["mask"].next()
                            n = tal["mask_ready"].next()
                            m = tal["mask_ready"].next()
                            dve.wait_ge(mask_full, tal["mask"].done(i))
                            nc.vector.tensor_scalar(ROWS[:, 1], ROWS[:, 0].bitcast(I32), 0.0, 1.0 / st.scale,
                                                    ALU.not_equal, ALU.mult).then_inc(mask_ready, 1)
                            dve.wait_ge(mask_ready, tal["mask_ready"].done(n))
                            nc.vector.tensor_scalar(ROWS[:, 0], ROWS[:, 1], st.scale * FILL, -FILL, ALU.mult,
                                                    ALU.add).then_inc(mask_ready, 1)
                        elif kind == "SCORE":
                            n = tal["s"].next()
                            qt = k % NT
                            if st.bias == "side" and k < NT:
                                i = tal["side_ready"].next()
                                dve.wait_ge(side_ready, tal["side_ready"].done(i))
                            if st.bias == "mask":
                                dve.wait_ge(conv_done, NT)
                            dve.wait_ge(s_full, tal["s"].done(n))
                            if st.bias:
                                gate()
                                nc.vector.tensor_tensor_reduce(
                                    out=PR[:, k % 4], in0=psS[:, n % 2], in1=FB[:, qt], scale=-st.scale, scalar=BIG,
                                    op0=ALU.add, op1=ALU.min, accum_out=MN[:, k:k + 1]).then_inc(s_evac, 1)
                            else:
                                nc.vector.tensor_scalar(PR[:, k % 4], psS[:, n % 2], -st.scale, None, ALU.mult, ALU.min,
                                                        accum_out=MN[:, k:k + 1]).then_inc(s_evac, 1)
                        elif kind == "RECIP":
                            n = tal["exp"].next()
                            dve.wait_ge(exp_done, tal["exp"].done(n))
                            nc.vector.reciprocal(RS[:, k:k + 1], SM[:, k:k + 1]).then_inc(recip_done, 1)
                        elif kind == "TURN":
                            h, qt = divmod(k, NT)
                            n = tal["t"].next()
                            i = tal["t_hi"].next()
                            dve.wait_ge(t_hi, tal["t_hi"].done(i))
                            hi, lo = (PT[h % 2][:, p, :, qt * P:(qt + 1) * P] for p in range(2))
                            nc.vector.tensor_tensor(lo, psT[:, n % 2].rearrange("p (k t) -> p k t", k=NT), f32(hi),
                                                    ALU.subtract).then_inc(t_evac, 1)
                        elif kind == "PV":
                            g, j = divmod(k, st.per_group)
                            n = tal["pv_half"].next()
                            og = OG[j * dk:(j + 1) * dk, :]
                            dve.wait_ge(pv_half, tal["pv_half"].done(n))
                            nc.vector.tensor_tensor(og, psV[0:dk, n % 2], og, ALU.add).then_inc(pv_evac, 1)
                            if j == st.per_group - 1:
                                i = tal["o_hi"].next()
                                col = COL[st.cols] + (0 if st.cols == "ZERO" else 2 * NG) + g
                                dve.wait_ge(o_hi, tal["o_hi"].done(i))
                                nc.vector.scalar_tensor_tensor(
                                    out=OT[:, 1, g], in0=OG[:, :], scalar=COLS[:, col:col + 1], in1=f32(OT[:, 0, g]),
                                    op0=ALU.add, op1=ALU.subtract).then_inc(o_lo, 1)
                        elif kind == "V":
                            n = tal["j"].next()
                            tal["j_own"].next()
                            i = tal["j_hi"].next()
                            v = VAL[:, k].rearrange("p (h c) -> p h c", c=2 * dk)
                            dve.wait_ge(j_hi, tal["j_hi"].done(i))
                            nc.vector.tensor_tensor(v[:, :, dk:2 * dk], psJ[:, n % 2].rearrange("p (h c) -> p h c", c=dk),
                                                    f32(v[:, :, 0:dk]), ALU.subtract).then_inc(j_evac, 1)
                        elif kind == "OUT":
                            n = tal["j"].next()
                            own = tal["j_own"].next()
                            i = tal["y"].next()
                            dve.wait_ge(j_full, tal["j"].done(n))
                            if st.cols != "ZERO":
                                m = tal["res"].next()
                                dve.wait_ge(res_ready, tal["res"].done(m))
                            else:
                                dve.wait_ge(y_full[k], tal["y"].done(i))
                            nc.vector.tensor_tensor(Y[:, k], psJ[:, n % 2], Y[:, k], ALU.add).then_inc(j_evac, 1)
                            if st.norm:
                                stats(k, j_evac, tal["j_own"].done(own))
                        elif kind == "NORM":
                            if st.norm:
                                normalise(k)
                            else:
                                dve.wait_ge(j_evac, tal["j_own"].done(tal["j_own"].n - 1))
                                dve.sem_inc(y_norm, 1)

                def body(prev, nxt):
                    for events in schedule(st, prev, nxt):
                        run(events)

                run(prologue(st))
                body(False, True)
                keep = ["x_hi", "s", "exp", "t_hi", "t", "pv_half", "o_hi", "j", "j_hi", "j_own", "y"]
                keep += ["mask", "mask_ready", "side_ready"] if st.bias == "side" else []
                keep += ["rstd", "y_sum"] if st.norm else []
                keep += ["res"] if st.cols != "ZERO" else []
                with loop(dve, B - 2, {k: tal[k] for k in keep},
                          dict(per, j_own=per["j"], mask_ready=2, y_sum=NT)):
                    body(True, True)
                body(True, False)
                run(drain(st))

            tal.update(h=Tally(h_full, credit=2), used=Tally(h_used, credit=2), acc=Tally(h_used, credit=2))
            acc = [psJ[:, 0], psJ[:, 1], psV[:, 0], psV[:, 1]]

            def hidden(f):
                n = tal["h"].next()
                i = tal["used"].next()
                dve.wait_ge(h_full, tal["h"].done(n))
                dve.wait_ge(h_used, tal["used"].done(i - 2))
                nc.vector.tensor_copy(HH[n % 2], HF[:, n % 2]).then_inc(h_hi, 1)

            def results():
                dve.wait_ge(h_used, tal["used"].done(tal["used"].n - 1))
                for tt in range(NT):
                    m = tal["res"].next()
                    own = tal["acc_own"].next()
                    dve.wait_ge(res_ready, tal["res"].done(m))
                    nc.vector.tensor_tensor(Y[:, tt], acc[tt], Y[:, tt], ALU.add).then_inc(acc_evac, 1)
                    stats(tt, acc_evac, tal["acc_own"].done(own))
                for tt in range(NT):
                    normalise(tt)

            for tt in range(NT):
                x_lo_part(tt)
            with loop(dve, B - 1, {k: tal[k] for k in ("x_hi", "t", "h", "used", "res", "acc_own", "rstd", "y_sum")},
                      dict(x_hi=NT, t=NT, h=NF, used=NF, res=NT, acc_own=NT, rstd=NT, y_sum=NT)):
                for f in range(NF):
                    hidden(f)
                for tt in range(NT):
                    x_lo_part(tt)
                results()
            for f in range(NF):
                hidden(f)
            results()

        @block.gpsimd
        def _(pool):
            tal = dict(cs_hi=Tally(cs_hi), recip=Tally(recip_done), side=RingTally(side_full),
                       mask_ready=Tally(mask_ready), side_half=Tally(side_half), y=RingTally(y_full), mv=Tally(mv_ready),
                       var=Tally(var_eps), y_norm=Tally(y_norm), gain=Tally(y_gain))
            nc.gpsimd.memset(ID[:, :], 0.0).then_inc(ident_zero, 1)
            pool.wait_ge(ident_zero, 1)
            nc.gpsimd.affine_select(out=ID[:, :], in_=ID[:, :], compare_op=ALU.not_equal, fill=1.0, base=0,
                                    pattern=[[-1, P]], channel_multiplier=1).then_inc(ident_ready, 1)
            pool.sem_inc(cs_lo, 2)
            pool.sem_inc(h_lo, 2)
            pool.wait_ge(const_ready, CONSTS)

            def gate():
                pool.sem_inc(gate_pool, 1)

            cs_turn = [0]

            def split_lo(dst, hi):
                n = tal["cs_hi"].next()
                pool.wait_ge(cs_hi, tal["cs_hi"].done(n))
                nc.gpsimd.tensor_tensor(dst, cs[:, n % 2], f32(hi), ALU.subtract).then_inc(cs_lo, 1)

            def residual(tt):
                i = tal["y"].next()
                pool.wait_ge(y_full[tt], tal["y"].done(i))
                nc.gpsimd.tensor_tensor(Y[:, tt], Y[:, tt], ROWS[:, 0], ALU.add).then_inc(res_ready, 1)

            def deviation(tt, eps):
                n = tal["mv"].next()
                i = tal["var"].next()
                pool.wait_ge(mv_ready, tal["mv"].done(n))
                nc.gpsimd.tensor_tensor(VE[:, tt:tt + 1], MV[:, tt, 1:2], CONST[:, EPS[eps]:EPS[eps] + 1],
                                        ALU.add).then_inc(var_eps, 1)
                pool.wait_ge(var_eps, tal["var"].done(i))
                nc.gpsimd.tensor_tensor(RD[:, tt:tt + 1], VE[:, tt:tt + 1], CONST[:, 0:1], ALU.pow).then_inc(rstd, 1)

            def gain_offset(tt):
                n = tal["y_norm"].next()
                i = tal["gain"].next()
                pool.wait_ge(y_norm, tal["y_norm"].done(n))
                nc.gpsimd.tensor_tensor(Y[:, tt], Y[:, tt], ROWS[:, 2], ALU.mult).then_inc(y_gain, 1)
                pool.wait_ge(y_gain, tal["gain"].done(i))
                nc.gpsimd.tensor_tensor(Y[:, tt], Y[:, tt], ROWS[:, 3], ALU.add).then_inc(y_done, 1)

            rows_seen = 16
            for st in STAGES:
                T, per = st.steps, counts(st)
                if st.rows:
                    rows_seen += 16 * (3 if st.cols != "ZERO" else 2)
                    pool.wait_ge(rows_full, rows_seen)
                for b in range(4):
                    for kt in range(KT):
                        split_lo(w_part(b, 1)[:, kt], w_part(b, 0)[:, kt])

                def run(events):
                    for kind, k in events:
                        if kind == "C":
                            split_lo(cT[:, 1, k], cT[:, 0, k])
                        elif kind == "ROWMASK":
                            tal["mask_ready"].next()
                            tal["mask_ready"].next()
                        elif kind == "SIDE":
                            i = tal["side"].next()
                            n = tal["side_half"].next()
                            pool.wait_ge(side_full[k], tal["side"].done(i))
                            if k == 0:
                                pool.wait_ge(mask_ready, tal["mask_ready"].done(tal["mask_ready"].n - 1))
                            nc.gpsimd.tensor_tensor(FB[:, k], FB[:, k], ROWS[:, 1], ALU.mult).then_inc(side_half, 1)
                            pool.wait_ge(side_half, tal["side_half"].done(n))
                            nc.gpsimd.tensor_tensor(FB[:, k], FB[:, k], ROWS[:, 0], ALU.add).then_inc(side_ready, 1)
                        elif kind == "RECIP":
                            n = tal["recip"].next()
                            pool.wait_ge(recip_done, tal["recip"].done(n))
                            gate()
                            nc.gpsimd.tensor_scalar(PR[:, k % 4], PR[:, k % 4], RS[:, k:k + 1], 1.0, ALU.mult,
                                                    ALU.mult).then_inc(p_ready, 1)
                        elif kind == "RES" and st.cols != "ZERO":
                            residual(k)
                        elif kind == "OUT" and st.norm:
                            deviation(k, st.eps)
                        elif kind == "NORM" and st.norm:
                            gain_offset(k)

                def body(prev, nxt):
                    for events in schedule(st, prev, nxt):
                        run(events)

                run(prologue(st))
                body(False, True)
                keep = ["recip"] + (["cs_hi"] if st.context else [])
                keep += ["side", "side_half", "mask_ready"] if st.bias == "side" else []
                keep += ["mv", "var", "y_norm", "gain"] if st.norm else []
                keep += ["y"] if st.cols != "ZERO" else []
                with loop(pool, B - 2, {k: tal[k] for k in keep}, dict(per, side_half=NT, mask_ready=2)):
                    body(True, True)
                body(True, False)
                run(drain(st))
                if not st.norm:
                    tal["y_norm"].n += B * NT
                if st.cols == "ZERO":
                    tal["y"].n += B * NT

            tal.update(h=Tally(h_hi))
            rows_seen += 48
            pool.wait_ge(rows_full, rows_seen)
            for b in range(8):
                for kt in range(KT):
                    split_lo(w_part(b, 1)[:, kt], w_part(b, 0)[:, kt])

            def hidden_lo(f):
                n = tal["h"].next()
                pool.wait_ge(h_hi, tal["h"].done(n))
                nc.gpsimd.tensor_tensor(HL[n % 2], HF[:, n % 2], f32(HH[n % 2]), ALU.subtract).then_inc(h_lo, 1)

            with loop(pool, B, {k: tal[k] for k in ("h", "y", "mv", "var", "y_norm", "gain")},
                      dict(h=NF, y=NT, mv=NT, var=NT, y_norm=NT, gain=NT)):
                for f in range(NF):
                    hidden_lo(f)
                    if f >= NF - NT:
                        residual(f - NF + NT)
                for tt in range(NT):
                    deviation(tt, FF_EPS)
                for tt in range(NT):
                    gain_offset(tt)


def kernel(**inputs):
    import numpy as np
    import concourse.bacc as bacc
    from concourse import mybir
    from concourse.bass_utils import run_bass_kernel_spmd

    a = {k: np.asarray(v) for k, v in inputs.items()}
    h = AD
    l0 = lambda k: a["L0_xattn_" + k]
    l1 = lambda k: a["L1_xattn_" + k]
    blocks = []
    for half in range(2):
        cut = slice(half * h, (half + 1) * h)
        blocks += [l0("w_q")[:, cut], l0("w_k")[:, cut], l0("w_v")[:, cut], l0("w_o")[cut, :]]
    for p in ("sa", "ca"):
        blocks += [l1(f"{p}_w{m}").T for m in "qkvo"]
    blocks += [l1("ff_w1")[i * 512:(i + 1) * 512, :].T for i in range(FF // 512)]
    blocks += [l1("ff_w2")[:, i * 512:(i + 1) * 512].T for i in range(FF // 512)]
    columns = lambda v: v.reshape(-1, P).T
    arrays = {
        "x": a["x"],
        "ctx_t": a["ctx_1024"].transpose(0, 2, 1),
        "side": a["fside_Bx1xSxS2_0"],
        "key_mask": a["mask_Bx1x1xS2_ik0"].reshape(B, 1, 1, S),
        "pair_mask": a["mask_1x1xSxS_ik0"],
        "w": np.stack(blocks),
        "rows": np.stack([
            np.stack([l0("ln_b"), l0("ln_g"), l0("ln_b")]),
            np.stack([l1("sa_bo"), l1("ln1_g"), l1("ln1_b")]),
            np.stack([l1("ca_bo"), l1("ln2_g"), l1("ln2_b")]),
            np.stack([l1("ff_b2"), l1("ln3_g"), l1("ln3_b")])]),
        "cols": np.concatenate([columns(l1(f"{p}_b{m}")) for p in ("sa", "ca") for m in "qkv"]
                               + [columns(l1("ff_b1"))], axis=1),
    }
    nc = bacc.Bacc("TRN2", target_bir_lowering=False, num_devices=1, dynamic_dma_scratch_size=1024)
    feed, aps = {}, []
    for name, v in arrays.items():
        v = np.ascontiguousarray(v)
        feed[f"in_{name}"] = v
        aps.append(nc.dram_tensor(f"in_{name}", v.shape, mybir.dt.from_np(v.dtype), kind="ExternalInput").ap())
    out = nc.dram_tensor("result", (B, S, D), mybir.dt.float32, kind="ExternalOutput").ap()
    build(nc, *aps, out)
    r = run_bass_kernel_spmd(nc, [feed], core_ids=[0])
    return r.results[0]["result"]
```

```python
from contextlib import ExitStack, contextmanager

B, S, D, FF = 8, 512, 512, 2048
P = 128
NT = S // P
KT = D // P
NF = FF // P
AD = 512
NG = AD // P

COL = {"SA": 0, "CA": 12, "FF": 24, "ZERO": 40}
NCOL = 40
CONSTS = 4
ROW = {"L0": 0, "SA": 1, "CA": 2, "FF": 3}


class Stage:

    def __init__(self, name, dk, block, src, res, dst, context, bias, norm, eps, rows, cols):
        self.name, self.dk, self.block = name, dk, block
        self.src, self.res, self.dst = src, res, dst
        self.context, self.bias, self.norm, self.eps = context, bias, norm, eps
        self.rows, self.cols = rows, cols
        self.heads = AD // dk
        self.per_group = P // dk
        self.steps = self.heads * NT
        self.scale = float(dk) ** -0.5


STAGES = [
    Stage("L0a", 64, 0, "x", "x", "half", True, "side", False, 0.0, None, "ZERO"),
    Stage("L0b", 64, 4, "x", "half", "x1", True, "side", True, 1e-6, "L0", "ZERO"),
    Stage("SA", 32, 8, "x1", "x1", "x2", False, "mask", True, 1e-5, "SA", "SA"),
    Stage("CA", 32, 12, "x2", "x2", "x3", True, None, True, 1e-5, "CA", "CA"),
]
FF_BLOCK, FF_EPS = 16, 1e-5


STEPS = [
    "P_LO",
    "X_LO",
    "PROB",
    "EXP",
    "SCORE",
    "SIDE",
    "MAX",
    "PV",
    "TURN",
    "X_TURN",
    "P_HI",
    "X_HI",
    "HEAD_LO",
    "HEAD_SUM",
    "GROUP_HI",
    "GROUP_LO",
    "J_HI",
    "J_LO",
    "C_HI",
    "C_LO",
    "RES",
    "OUT_SUM",
    "NORM",
    "ROWMASK",
    "JOB",
    "LOAD_X", "LOAD_C", "LOAD_MASK", "LOAD_SIDE", "LOAD_RES",
    "STORE",
]


def timetable(st):
    T, NH = st.steps, st.heads
    wide = st.dk == 64
    ev = []

    def add(slot, step, what=0):
        ev.append((slot, step, what))

    def job(name, slots):
        for part, slot in enumerate(slots):
            add(slot, "JOB", (name, part))
        if name[0] != "OUT":
            add(slots[-1] + 1, "J_HI", name)
            add(slots[-1] + 1, "J_LO", name)

    for s in range(T):
        add(s, "SCORE", s)
        add(s, "MAX", s)
        add(s + 1, "EXP", s)
        add(s + 2, "PROB", s)
        add(s + 3, "TURN", s)
        add(s + 3, "P_HI", s)
        add(s + 4, "P_LO", s)
    for h in range(NH):
        for kt in range(NT):
            add(NT * h + 8 + kt, "PV", (h, kt))
        add(NT * h + 12, "HEAD_LO", h)
        add(NT * h + 13, "HEAD_SUM", h)
        if h % st.per_group == st.per_group - 1:
            add(NT * h + 14, "GROUP_HI", h // st.per_group)
            add(NT * h + 15, "GROUP_LO", h // st.per_group)
    span = T // NG
    for g in range(NG):
        at = span * (g - 1) + (0 if wide else 7)
        if wide and g == 2:
            job(("Q", g), [at] * 4)
            job(("K", g), [at + 1] * 4)
        else:
            job(("Q", g), [at, at, at + 1, at + 1])
            job(("K", g), [at + 2, at + 2, at + 3, at + 3])
    if wide:
        job(("V", 0, 0), [4, 4, 5, 5])
        job(("V", 0, 1), [6, 6, 7, 7])
        job(("V", 1, 0), [10] * 4)
        job(("V", 1, 1), [11] * 4)
    else:
        job(("V", 0, 0), [0, 0, 1, 2])
        job(("V", 0, 1), [3, 4, 5, 6])
        job(("V", 1, 0), [27, 28, 29, 30])
        job(("V", 1, 1), [31, 32, 33, 34])
    for tt in range(NT):
        x_at = -12 + tt if wide else -21 + tt + 2 * (tt // 2)
        add(x_at, "X_TURN", tt)
        add(x_at, "X_HI", tt)
        add(x_at + 1, "X_LO", tt)
        add(x_at - 6 if tt < 2 else x_at - (1 if wide else 3), "LOAD_X", tt)
        if st.context:
            c_at = x_at + (tt // 2 if wide else 1)
            add(c_at, "C_HI", tt)
            add(c_at + 1, "C_LO", tt)
            add(c_at - 7 if tt < 2 else c_at - 2, "LOAD_C", tt)
        step = 1 if wide else 2
        out = T + 12 + step * tt
        job(("OUT", tt), [out] * 4 if wide else [out, out, out + 1, out + 1])
        add(T + 4 + tt, "LOAD_RES", tt)
        add(T + 8 + tt, "RES", tt)
        add(out + step, "OUT_SUM", tt)
        add(out + step + 2, "NORM", tt)
        add(out + step + 3, "STORE", tt)
        if st.bias == "side":
            add(tt - 4, "LOAD_SIDE", tt)
            add(tt - 1, "SIDE", tt)
    if st.bias == "side":
        add(-10, "LOAD_MASK")
        add(-6, "ROWMASK")
    return sorted(ev, key=lambda e: (e[0], STEPS.index(e[1])))


def body_steps(st, prev, nxt):
    T = st.steps
    ev = []
    for slot, step, what in timetable(st):
        off = -1 if slot >= T else 1 if slot < 0 else 0
        if off == 0 or (prev if off < 0 else nxt):
            ev.append((slot % T, STEPS.index(step), step, what, off))
    return [e[2:] for e in sorted(ev, key=lambda e: e[:2])]


def prologue(st):
    return [(step, what, 0) for slot, step, what in timetable(st) if slot < 0]


def drain(st):
    return [(step, what, 0) for slot, step, what in timetable(st) if slot >= st.steps]


class Tally:

    def __init__(self, sem, unit=1, credit=0):
        self.sem, self.unit, self.credit = sem, unit, credit
        self.n, self.per, self.turn, self.marks = 0, 0, None, {}

    def next(self):
        self.n += 1
        return self.n - 1

    def mark(self, name):
        self.marks[name] = self.n - 1

    def marked(self, name):
        return self.marks.get(name)

    def done(self, n):
        v = self.unit * (n + 1) + self.credit
        return v if self.turn is None else self.turn * (self.per * self.unit) + v


class RingTally(Tally):

    def __init__(self, sems, unit=16, credit=0):
        Tally.__init__(self, None, unit, credit)
        self.sems = sems

    def slot(self, n):
        return n % len(self.sems)

    def sem_of(self, n):
        return self.sems[n % len(self.sems)]

    def done(self, n):
        R = len(self.sems)
        v = self.unit * (n // R + 1) + self.credit
        return v if self.turn is None else self.turn * (self.per // R * self.unit) + v


@contextmanager
def turns(eng, count, tallies):
    first = [t.n for t, _ in tallies]
    with eng.Fori(0, count) as r:
        for t, per in tallies:
            t.per, t.turn = per, r
        yield r
    for (t, per), n in zip(tallies, first):
        assert t.n - n == per, (t.sem, t.n - n, per)
        t.turn = None
        t.n += per * (count - 1)
        t.marks = {k: v + per * (count - 1) for k, v in t.marks.items()}


def build(nc, x, ctx_t, side, key_mask, pair_mask, w, rows, cols, out):
    import concourse.bass as bass
    from concourse import mybir

    F32, F32R, I32 = mybir.dt.float32, mybir.dt.float32r, mybir.dt.int32
    ALU, ACT = mybir.AluOpType, mybir.ActivationFunctionType
    BIG = 3.0e38
    FILL = 1.0e30

    dram = {"x": x, "out": out}
    for name in ("half", "x1", "x2", "x3"):
        dram[name] = nc.dram_tensor(name, (B, S, D), F32, kind="Internal").ap()

    with ExitStack() as stack:
        def sb(name, shape, dt=F32):
            return stack.enter_context(nc.sbuf_tensor(name, shape, dt))

        def sem(name):
            return stack.enter_context(nc.semaphore(name))

        W = sb("W", [P, 8, KT, D], F32R)
        R = sb("R", [P, 8, KT, D], F32R)
        cT = R[:, 0:2]
        VAL = R[:, 2:4].rearrange("p a k n -> p (a k n)").rearrange("p (k n) -> p k n", k=NT)
        PT = [R[:, 4 + 2 * i:6 + 2 * i] for i in range(2)]
        xT = sb("xT", [P, 2, KT, S], F32R)
        xs = sb("xs", [P, 2, D])
        cs = sb("cs", [P, 2, S])
        QK = sb("QK", [P, 2, 4, S], F32R)
        PR = sb("PR", [P, 4, S])
        FB = sb("FB", [P, NT, S])
        OT = sb("OT", [P, 2, NG, S], F32R)
        OG = sb("OG", [P, S])
        Y = sb("Y", [P, NT, D])
        ROWS = sb("ROWS", [P, 3, D])
        COLS = sb("COLS", [P, NCOL + NG])
        MN = sb("MN", [P, 8])
        SM = sb("SM", [P, 8])
        RS = sb("RS", [P, 8])
        ID = sb("ID", [P, P])
        ST = sb("ST", [P, NT, 6])
        MV = sb("MV", [P, NT, 2])
        VE = sb("VE", [P, NT])
        RD = sb("RD", [P, NT])
        CONST = sb("CONST", [P, 3])
        EPS = {1e-6: 1, 1e-5: 2}
        HF = PR
        HH, HL = QK[:, 0], QK[:, 1]

        psS = stack.enter_context(nc.psum_tensor("psS", [P, 2, 512], F32))
        psT = stack.enter_context(nc.psum_tensor("psT", [P, 2, 512], F32))
        psJ = stack.enter_context(nc.psum_tensor("psJ", [P, 2, 512], F32))
        psV = stack.enter_context(nc.psum_tensor("psV", [P, 2, 512], F32))

        xs_full = [sem(f"xs_full{i}") for i in range(2)]
        ws_full = [sem(f"ws_full{i}") for i in range(2)]
        cs_full = [sem(f"cs_full{i}") for i in range(2)]
        side_full = [sem(f"side_full{i}") for i in range(NT)]
        mask_full = sem("mask_full")
        rows_full = sem("rows_full")
        y_full = [sem(f"y_full{i}") for i in range(NT)]
        y_stored = [sem(f"y_stored{i}") for i in range(NT)]
        const_ready = sem("const_ready")
        ident_ready = sem("ident_ready")
        ident_zero = sem("ident_zero")
        x_hi = sem("x_hi")
        w_hi = sem("w_hi")
        w_lo = sem("w_lo")
        cs_hi = sem("cs_hi")
        cs_lo = sem("cs_lo")
        s_full = sem("s_full")
        s_evac = sem("s_evac")
        exp_done = sem("exp_done")
        recip_done = sem("recip_done")
        p_ready = sem("p_ready")
        t_full = sem("t_full")
        t_hi = sem("t_hi")
        t_evac = sem("t_evac")
        pv_full = sem("pv_full")
        pv_half = sem("pv_half")
        pv_evac = sem("pv_evac")
        o_hi = sem("o_hi")
        o_lo = sem("o_lo")
        j_full = sem("j_full")
        j_hi = sem("j_hi")
        j_evac = sem("j_evac")
        mask_ready = sem("mask_ready")
        side_ready = sem("side_ready")
        res_ready = sem("res_ready")
        mv_ready = sem("mv_ready")
        var_eps = sem("var_eps")
        rstd = sem("rstd")
        y_norm = sem("y_norm")
        y_gain = sem("y_gain")
        y_done = sem("y_done")
        y_sum = sem("y_sum")
        conv_done = sem("conv_done")
        u_full = sem("u_full")
        h_full = sem("h_full")
        h_hi = sem("h_hi")
        h_lo = sem("h_lo")
        h_used = sem("h_used")
        acc_evac = sem("acc_evac")
        gate_dve = sem("gate_dve")
        gate_pool = sem("gate_pool")

        def w_part(b, part):
            return (W if b < 4 else R)[:, 2 * (b % 4) + part]

        def f32(ap):
            return ap.bitcast(F32)

        def counts(st):
            T, H = st.steps, st.heads
            return dict(xs=NT, x_hi=NT, cs=KT, cs_hi=KT, cs_lo=KT, s=T, s_full=T, exp=T, recip=T, p=T, t=T + NT, t_hi=T,
                        pv=H, pv_half=H, pv_evac=H, o_hi=NG, o_lo=NG, j=2 * NG + 2 * NT, j_own=2 * NG + 2 * NT,
                        j_hi=2 * NG + NT, mask=1, mask_ready=1, side=NT, side_ready=NT, res=NT, y=NT, mv=NT,
                        var=NT, rstd=NT, y_norm=NT, gain=NT, y_done=NT, y_sum=NT)

        def bias_col(st, which, g):
            return COL[st.cols] + (0 if st.cols == "ZERO" else "QKV".index(which) * NG) + g

        def value_part(st, name, part):
            half, pair, n = name[1], name[2], st.heads // 2
            v = VAL[:, 2 * pair:2 * pair + 2].rearrange("p t (h c) -> p t h c", c=2 * st.dk)
            return v[:, :, half * n:(half + 1) * n, part * st.dk:(part + 1) * st.dk]

        def projected(st, n):
            return psJ[:, n % 2].rearrange("p (t h c) -> p t h c", t=2, c=st.dk)

        def new_stage(tal, st):
            for t in tal.values():
                t.marks.clear()

        def stage_loop(eng, tal, st, names, run):
            per = counts(st)
            names = names + (["cs", "cs_hi", "cs_lo"] if st.context else [])
            names = names + (["mask", "mask_ready", "side", "side_ready"] if st.bias == "side" else [])
            names = names + (["mv", "var", "rstd", "gain", "y_sum", "y_done"] if st.norm else [])
            names = names + (["res"] if st.cols != "ZERO" else [])
            run(prologue(st), 0)
            run(body_steps(st, False, True), 0)
            with turns(eng, B - 2, [(tal[k], per[k]) for k in dict.fromkeys(names) if k in tal]) as r:
                run(body_steps(st, True, True), r + 1)
            run(body_steps(st, True, False), B - 1)
            run(drain(st), B - 1)

        block = stack.enter_context(nc.Block())

        @block.sync
        def _(sp):
            tal = dict(xs=RingTally(xs_full), x_hi=Tally(x_hi, credit=2), cs=RingTally(cs_full),
                       cs_lo=Tally(cs_lo, credit=2), ws=RingTally(ws_full), w_lo=Tally(w_lo, credit=2),
                       s=Tally(s_evac, credit=2), side=RingTally(side_full), side_ready=Tally(side_ready),
                       y=RingTally(y_stored, credit=16), y_norm=Tally(y_norm), y_done=Tally(y_done))
            for tt in range(NT):
                sp.sem_inc(y_stored[tt], 16)
            sp.dma_start(COLS[:, 0:NCOL], cols).then_inc(rows_full, 16)

            def load_x(src, b, tt):
                n = tal["x_hi"].next()
                sp.wait_ge(x_hi, tal["x_hi"].done(n - 2))
                i = tal["xs"].next()
                sp.dma_start(xs[:, tal["xs"].slot(i)], dram[src][b, tt * P:(tt + 1) * P, :]).then_inc(
                    tal["xs"].sem_of(i), 16)

            def load_w(src):
                n = tal["w_lo"].next()
                sp.wait_ge(w_lo, tal["w_lo"].done(n - 2))
                i = tal["ws"].next()
                sp.dma_start(xs[:, tal["ws"].slot(i)], src).then_inc(tal["ws"].sem_of(i), 16)

            def load_c(st, b, tt):
                n = tal["cs_lo"].next()
                sp.wait_ge(cs_lo, tal["cs_lo"].done(n - 2))
                i = tal["cs"].next()
                sp.dma_start(cs[:, tal["cs"].slot(i)], ctx_t[b, tt * P:(tt + 1) * P, :]).then_inc(
                    tal["cs"].sem_of(i), 16)

            def load_res(res, b, tt):
                i = tal["y"].next()
                sp.wait_ge(y_stored[tt], tal["y"].done(i - NT))
                sp.dma_start(Y[:, tt], dram[res][b, tt * P:(tt + 1) * P, :]).then_inc(y_full[tt], 16)

            def store(name, norm, b, tt):
                which, ready = ("y_done", y_done) if norm else ("y_norm", y_norm)
                n = tal[which].next()
                sp.wait_ge(ready, tal[which].done(n))
                sp.dma_start(dram[name][b, tt * P:(tt + 1) * P, :], Y[:, tt]).then_inc(y_stored[tt], 16)

            def begin(rows, bias_row, blocks):
                if tal["y"].n:
                    for tt in range(NT):
                        sp.wait_ge(y_stored[tt], tal["y"].done(tal["y"].n - NT + tt))
                if rows is not None:
                    for k in range(0 if bias_row else 1, 3):
                        sp.dma_start(ROWS[:, k], rows_d(rows, k)).then_inc(rows_full, 16)
                for b in blocks:
                    for kt in range(KT):
                        load_w(w[b, kt * P:(kt + 1) * P, :])
                sp.wait_ge(w_lo, tal["w_lo"].done(tal["w_lo"].n - 1))

            def rows_d(name, k):
                return rows[ROW[name], k:k + 1, :].to_broadcast([P, D])

            for st in STAGES:
                new_stage(tal, st)
                begin(st.rows, st.cols != "ZERO", range(st.block, st.block + 4))
                if st.bias == "mask":
                    for qt in range(NT):
                        i = tal["side"].next()
                        sp.dma_start(FB[:, qt].bitcast(I32), pair_mask[0, 0, qt * P:(qt + 1) * P, :]).then_inc(
                            tal["side"].sem_of(i), 16)

                def run(steps, batch):
                    for step, k, off in steps:
                        b = batch + off
                        if step == "MAX":
                            tal["s"].next()
                            tal["s"].mark(k)
                        elif step == "SIDE":
                            tal["side_ready"].next()
                            tal["side_ready"].mark(k)
                        elif step == "LOAD_X":
                            load_x(st.src, b, k)
                        elif step == "LOAD_C":
                            load_c(st, b, k)
                        elif step == "LOAD_MASK":
                            last = tal["side_ready"].marked(NT - 1)
                            if last is not None:
                                sp.wait_ge(side_ready, tal["side_ready"].done(last))
                            sp.dma_start(ROWS[:, 0].bitcast(I32), key_mask[b, 0, 0:1, :].to_broadcast([P, S])).then_inc(
                                mask_full, 16)
                        elif step == "LOAD_SIDE":
                            i = tal["side"].next()
                            last = tal["s"].marked(st.steps - NT + k)
                            if last is not None:
                                sp.wait_ge(s_evac, tal["s"].done(last))
                            sp.dma_start(FB[:, k], side[b, 0, k * P:(k + 1) * P, :]).then_inc(tal["side"].sem_of(i), 16)
                        elif step == "LOAD_RES":
                            load_res(st.res, b, k)
                        elif step == "STORE":
                            store(st.dst, st.norm, b, k)

                stage_loop(sp, tal, st, ["xs", "x_hi", "s", "y"] +
                           ([] if st.norm else ["y_norm"]), run)
                if st.norm:
                    tal["y_norm"].n += B * NT

            begin("FF", True, range(FF_BLOCK, FF_BLOCK + 8))

            def ff_inputs(b):
                for tt in range(NT):
                    load_x("x3", b, tt)

            def ff_residuals(b):
                for tt in range(NT):
                    load_res("x3", b, tt)

            def ff_stores(b):
                for tt in range(NT):
                    store("out", True, b, tt)

            ff_inputs(0)
            with turns(sp, B - 1, [(tal[k], NT) for k in ("xs", "x_hi", "y", "y_done")]) as r:
                ff_residuals(r)
                ff_inputs(r + 1)
                ff_stores(r)
            ff_residuals(B - 1)
            ff_stores(B - 1)
            for tt in range(NT):
                sp.wait_ge(y_stored[tt], tal["y"].done(tal["y"].n - NT + tt))

        @block.tensor
        def _(pe):
            tal = dict(xs=RingTally(xs_full), w_lo=Tally(w_lo, credit=2), cs_lo=Tally(cs_lo, credit=2), s=Tally(s_evac, credit=2),
                       p=Tally(p_ready), t=Tally(t_evac, credit=2), pv=Tally(pv_evac, credit=2),
                       o_lo=Tally(o_lo, credit=1), j=Tally(j_evac, credit=2))
            pe.sem_inc(h_used, 4)
            pe.wait_ge(ident_ready, 1)

            def three(dst, a, b, first=True, last=True):
                nc.tensor.matmul(dst, a[0], b[0], start=first, stop=False)
                nc.tensor.matmul(dst, a[0], b[1], start=False, stop=False)
                return nc.tensor.matmul(dst, a[1], b[0], start=False, stop=last)

            def parts(t, kt, cols):
                return [t[:, p, kt, cols] for p in range(2)]

            def w_parts(b, kt, cols):
                return [w_part(b, p)[:, kt, cols] for p in range(2)]

            def x_turn(tt):
                i = tal["xs"].next()
                n = tal["t"].next()
                pe.wait_ge(tal["xs"].sem_of(i), tal["xs"].done(i))
                pe.wait_ge(t_evac, tal["t"].done(n - 2))
                for kt in range(KT):
                    mm = nc.tensor.transpose(psT[:, n % 2, kt * P:(kt + 1) * P],
                                             xs[:, tal["xs"].slot(i), kt * P:(kt + 1) * P], ID[:, :])
                mm.then_inc(t_full, 1)
                return n

            def weights(count):
                for _ in range(count):
                    n = tal["w_lo"].next()
                pe.wait_ge(w_lo, tal["w_lo"].done(n))

            for st in STAGES:
                dk = st.dk
                src = cT if st.context else xT
                new_stage(tal, st)
                weights(4 * KT)

                def score(k):
                    h, qt = divmod(k, NT)
                    n = tal["s"].next()
                    g, j = divmod(h, st.per_group)
                    if j == 0 and qt == 0:
                        pe.wait_ge(j_evac, tal["j"].done(tal["j"].marked(("K", g))))
                    pe.wait_ge(s_evac, tal["s"].done(n - 2))
                    qk = QK[j * dk:(j + 1) * dk, g % 2]
                    q = [qk[:, p, qt * P:(qt + 1) * P] for p in range(2)]
                    three(psS[:, n % 2], q, [qk[:, 2], qk[:, 3]]).then_inc(s_full, 1)

                def turn(k):
                    n = tal["t"].next()
                    i = tal["p"].next()
                    pe.wait_ge(p_ready, tal["p"].done(i))
                    pe.wait_ge(t_evac, tal["t"].done(n - 2))
                    for kt in range(NT):
                        mm = nc.tensor.transpose(psT[:, n % 2, kt * P:(kt + 1) * P], PR[:, k % 4, kt * P:(kt + 1) * P],
                                                 ID[:, :])
                    mm.then_inc(t_full, 1)
                    tal["t"].mark(("turned", k))

                def values(h, kt):
                    if kt == 0:
                        n = tal["pv"].next()
                        pe.wait_ge(t_evac, tal["t"].done(tal["t"].marked(("turned", NT * h + NT - 1))))
                        pe.wait_ge(pv_evac, tal["pv"].done(n - 2))
                    n = tal["pv"].n - 1
                    if h % (st.heads // 2) == 0 and kt % 2 == 0:
                        made = tal["j"].marked(("V", h // (st.heads // 2), kt // 2))
                        pe.wait_ge(j_evac, tal["j"].done(made))
                    for p in range(2):
                        mm = nc.tensor.matmul(psV[0:2 * dk, n % 2], VAL[:, kt, 2 * dk * h:2 * dk * (h + 1)],
                                              PT[h % 2][:, p, kt, :], start=(kt == 0 and p == 0),
                                              stop=(kt == NT - 1 and p == 1))
                    if kt == NT - 1:
                        mm.then_inc(pv_full, 1)

                def job(name, part):
                    if part == 0:
                        n = tal["j"].next()
                        tal["j"].mark(name)
                        if name == ("Q", 0):
                            pe.wait_ge(t_evac, tal["t"].done(tal["t"].marked(("x", NT - 1))))
                        if name == ("K", 0) and st.context:
                            pe.wait_ge(cs_lo, tal["cs_lo"].done(tal["cs_lo"].marked(NT - 1)))
                        if name == ("OUT", 0):
                            pe.wait_ge(o_lo, tal["o_lo"].done(tal["o_lo"].marked(NG - 1)))
                        pe.wait_ge(j_evac, tal["j"].done(n - 2))
                    n = tal["j"].n - 1
                    kind, last = name[0], part == KT - 1
                    if kind in "QK":
                        cols = slice(name[1] * P, (name[1] + 1) * P)
                        data, b = (xT, 0) if kind == "Q" else (src, 1)
                        mm = three(psJ[:, n % 2], w_parts(b, part, cols), parts(data, part, slice(0, S)), part == 0, last)
                    elif kind == "OUT":
                        tile = slice(name[1] * P, (name[1] + 1) * P)
                        mm = three(psJ[:, n % 2], parts(OT, part, tile), w_parts(3, part, slice(0, D)), part == 0, last)
                    else:
                        half, which = AD // 2, part // 2
                        tile = slice((2 * name[2] + which) * P, (2 * name[2] + which + 1) * P)
                        for kt in (0, 1) if part % 2 == 0 else (2, 3):
                            mm = three(psJ[:, n % 2, which * half:(which + 1) * half], parts(src, kt, tile),
                                       w_parts(2, kt, slice(name[1] * half, (name[1] + 1) * half)), kt == 0, kt == KT - 1)
                    if last:
                        mm.then_inc(j_full, 1)

                def run(steps, batch):
                    for step, k, _ in steps:
                        if step == "SCORE":
                            score(k)
                        elif step == "TURN":
                            turn(k)
                        elif step == "X_TURN":
                            x_turn(k)
                            tal["t"].mark(("x", k))
                        elif step == "PV":
                            values(*k)
                        elif step == "JOB":
                            job(*k)
                        elif step == "C_LO":
                            tal["cs_lo"].next()
                            tal["cs_lo"].mark(k)
                        elif step == "GROUP_LO":
                            tal["o_lo"].next()
                            tal["o_lo"].mark(k)

                stage_loop(pe, tal, st, ["xs", "s", "p", "t", "pv", "o_lo", "j"], run)

            tal.update(u=Tally(h_full, credit=2), h=Tally(h_lo, credit=4), acc=Tally(acc_evac, credit=NT))
            weights(8 * KT)
            acc = [psJ[:, 0], psJ[:, 1], psV[:, 0], psV[:, 1]]

            def up(f, x_last):
                n = tal["u"].next()
                if f == 0:
                    pe.wait_ge(t_evac, tal["t"].done(x_last))
                pe.wait_ge(h_full, tal["u"].done(n - 2))
                for kt in range(KT):
                    mm = three(psS[:, n % 2], w_parts(f // 4, kt, slice((f % 4) * P, (f % 4 + 1) * P)),
                               parts(xT, kt, slice(0, S)), kt == 0, kt == KT - 1)
                mm.then_inc(u_full, 1)

            def down(f):
                n = tal["h"].next()
                pe.wait_ge(h_lo, tal["h"].done(n))
                if f == 0:
                    for tt in range(NT):
                        i = tal["acc"].next()
                    pe.wait_ge(acc_evac, tal["acc"].done(i - NT))
                for tt in range(NT):
                    h = [t[:, n % 4, tt * P:(tt + 1) * P] for t in (HH, HL)]
                    mm = three(acc[tt], h, w_parts(4 + f // 4, f % 4, slice(0, D)), f == 0, f == NF - 1)
                mm.then_inc(h_used, 1)

            def ff(x_last, nxt):
                up(0, x_last)
                up(1, None)
                for f in range(2, NF):
                    up(f, None)
                    down(f - 2)
                for f in range(2):
                    if nxt:
                        x_turn(2 * f)
                        x_turn(2 * f + 1)
                    down(NF - 2 + f)

            for tt in range(NT):
                x_turn(tt)
            with turns(pe, B - 1, [(tal["xs"], NT), (tal["t"], NT), (tal["u"], NF), (tal["h"], NF), (tal["acc"], NT)]):
                ff(tal["t"].n - 1, True)
            ff(tal["t"].n - 1, False)

        @block.scalar
        def _(act):
            tal = dict(ws=RingTally(ws_full), cs=RingTally(cs_full), t=Tally(t_full), s=Tally(s_evac, credit=2), pv=Tally(pv_full),
                       o_lo=Tally(o_lo, credit=1), pv_evac=Tally(pv_evac, credit=2), j=Tally(j_full))
            act.sem_inc(x_hi, 2)
            act.sem_inc(h_full, 2)
            act.wait_ge(const_ready, CONSTS)
            act.wait_ge(rows_full, 16)

            def split_hi(dst, src, which, done):
                i = tal[which].next()
                act.wait_ge(tal[which].sem_of(i), tal[which].done(i))
                nc.scalar.activation(dst, src[:, tal[which].slot(i)], ACT.Copy).then_inc(done, 1)

            def x_hi_part(tt):
                n = tal["t"].next()
                act.wait_ge(t_full, tal["t"].done(n))
                nc.scalar.activation(xT[:, 0, :, tt * P:(tt + 1) * P],
                                     psT[:, n % 2].rearrange("p (k t) -> p k t", k=KT), ACT.Copy).then_inc(x_hi, 1)

            for st in STAGES:
                dk = st.dk
                new_stage(tal, st)
                for b in range(4):
                    for kt in range(KT):
                        split_hi(w_part(b, 0)[:, kt], xs, "ws", w_hi)

                def projection_hi(name):
                    n = tal["j"].next()
                    tal["j"].mark(name)
                    kind, g = name[0], name[1]
                    act.wait_ge(j_full, tal["j"].done(n))
                    if kind in "QK":
                        col = bias_col(st, kind, g)
                        nc.scalar.activation(QK[:, g % 2, 2 * "QK".index(kind)], psJ[:, n % 2], ACT.Identity,
                                             bias=COLS[:, col:col + 1]).then_inc(j_hi, 1)
                    else:
                        nc.scalar.activation(value_part(st, name, 0), projected(st, n), ACT.Copy).then_inc(j_hi, 1)

                def head_lo(h):
                    g, j = divmod(h, st.per_group)
                    n = tal["pv"].next()
                    act.wait_ge(pv_full, tal["pv"].done(n))
                    if j == 0:
                        i = tal["o_lo"].next()
                        act.wait_ge(o_lo, tal["o_lo"].done(i - 1))
                    nc.scalar.activation(OG[j * dk:(j + 1) * dk, :], psV[dk:2 * dk, n % 2], ACT.Copy).then_inc(pv_half, 1)

                def group_hi(g):
                    last = tal["j"].marked(("OUT", NT - 1))
                    if g == 0 and last is not None:
                        act.wait_ge(j_full, tal["j"].done(last))
                    col = bias_col(st, "V", g)
                    act.wait_ge(pv_evac, tal["pv_evac"].done(tal["pv_evac"].n - 1))
                    nc.scalar.activation(OT[:, 0, g], OG[:, :], ACT.Identity, bias=COLS[:, col:col + 1]).then_inc(o_hi, 1)

                def run(steps, batch):
                    for step, k, _ in steps:
                        if step == "EXP":
                            n = tal["s"].next()
                            act.wait_ge(s_evac, tal["s"].done(n))
                            nc.scalar.activation(PR[:, k % 4], PR[:, k % 4], ACT.Exp, bias=MN[:, k % 8:k % 8 + 1], scale=-1.0,
                                                 accum_out=SM[:, k % 8:k % 8 + 1]).then_inc(exp_done, 1)
                        elif step == "P_HI":
                            h, qt = divmod(k, NT)
                            n = tal["t"].next()
                            act.wait_ge(t_full, tal["t"].done(n))
                            nc.scalar.activation(PT[h % 2][:, 0, :, qt * P:(qt + 1) * P],
                                                 psT[:, n % 2].rearrange("p (k t) -> p k t", k=NT), ACT.Copy).then_inc(t_hi, 1)
                        elif step == "X_HI":
                            x_hi_part(k)
                        elif step == "C_HI":
                            split_hi(cT[:, 0, k], cs, "cs", cs_hi)
                        elif step == "HEAD_LO":
                            head_lo(k)
                        elif step == "HEAD_SUM":
                            tal["pv_evac"].next()
                        elif step == "GROUP_HI":
                            group_hi(k)
                        elif step == "J_HI":
                            projection_hi(k)
                        elif step == "OUT_SUM":
                            tal["j"].next()
                            tal["j"].mark(("OUT", k))

                stage_loop(act, tal, st, ["t", "s", "pv", "o_lo", "pv_evac", "j"], run)

            tal.update(u=Tally(u_full), h=Tally(h_lo, credit=4))
            for b in range(8):
                for kt in range(KT):
                    split_hi(w_part(b, 0)[:, kt], xs, "ws", w_hi)

            def relu(f):
                n = tal["u"].next()
                i = tal["h"].next()
                act.wait_ge(u_full, tal["u"].done(n))
                act.wait_ge(h_lo, tal["h"].done(i - 4))
                nc.scalar.activation(HF[:, n % 4], psS[:, n % 2], ACT.Relu,
                                     bias=COLS[:, COL["FF"] + f:COL["FF"] + f + 1]).then_inc(h_full, 1)

            for tt in range(NT):
                x_hi_part(tt)
            with turns(act, B - 1, [(tal["t"], NT), (tal["u"], NF), (tal["h"], NF)]):
                for f in range(NF):
                    relu(f)
                for tt in range(NT):
                    x_hi_part(tt)
            for f in range(NF):
                relu(f)

        @block.vector
        def _(dve):
            tal = dict(x_hi=Tally(x_hi, credit=2), w_hi=Tally(w_hi), cs_hi=Tally(cs_hi), s=Tally(s_full), exp=Tally(exp_done),
                       t_hi=Tally(t_hi), t=Tally(t_full), pv_half=Tally(pv_half), pv=Tally(pv_full), o_hi=Tally(o_hi),
                       j=Tally(j_full), j_hi=Tally(j_hi), j_own=Tally(j_evac, credit=2),
                       acc_own=Tally(acc_evac, credit=NT), mask=Tally(mask_full, unit=16), side=RingTally(side_full),
                       side_ready=Tally(side_ready), y=RingTally(y_full), res=Tally(res_ready), rstd=Tally(rstd),
                       y_sum=Tally(y_sum), mask_ready=Tally(mask_ready))
            nc.vector.memset(CONST[:, 0:1], -0.5).then_inc(const_ready, 1)
            nc.vector.memset(CONST[:, 1:2], 1e-6).then_inc(const_ready, 1)
            nc.vector.memset(CONST[:, 2:3], 1e-5).then_inc(const_ready, 1)
            nc.vector.memset(COLS[:, NCOL:NCOL + NG], 0.0).then_inc(const_ready, 1)
            dve.sem_inc(s_evac, 2)
            dve.sem_inc(t_evac, 2)
            dve.sem_inc(pv_evac, 2)
            dve.sem_inc(j_evac, 2)
            dve.sem_inc(o_lo, 1)
            dve.sem_inc(acc_evac, NT)
            dve.sem_inc(w_lo, 2)
            dve.sem_inc(cs_lo, 2)
            dve.sem_inc(h_lo, 4)

            def gate():
                dve.sem_inc(gate_dve, 1)

            def x_lo_part(tt):
                n = tal["t"].next()
                i = tal["x_hi"].next()
                dve.wait_ge(x_hi, tal["x_hi"].done(i))
                hi, lo = (xT[:, p, :, tt * P:(tt + 1) * P] for p in range(2))
                nc.vector.tensor_tensor(lo, psT[:, n % 2].rearrange("p (k t) -> p k t", k=KT), f32(hi),
                                        ALU.subtract).then_inc(t_evac, 1)

            def split_lo(dst, hi, src, which, split, done):
                n = tal[which].next()
                dve.wait_ge(split, tal[which].done(n))
                nc.vector.tensor_tensor(dst, src[:, n % 2], f32(hi), ALU.subtract).then_inc(done, 1)

            def stats(tt, wait_sem, wait_value):
                dve.wait_ge(wait_sem, wait_value)
                n = tal["y_sum"].next()
                nc.vector.bn_stats(ST[:, tt], Y[:, tt]).then_inc(y_sum, 1)
                dve.wait_ge(y_sum, tal["y_sum"].done(n))
                gate()
                nc.vector.bn_aggr(MV[:, tt], ST[:, tt]).then_inc(mv_ready, 1)

            def normalise(tt):
                n = tal["rstd"].next()
                dve.wait_ge(rstd, tal["rstd"].done(n))
                nc.vector.tensor_scalar(Y[:, tt], Y[:, tt], MV[:, tt, 0:1], RD[:, tt:tt + 1], ALU.subtract,
                                        ALU.mult).then_inc(y_norm, 1)

            for st in STAGES:
                dk = st.dk
                new_stage(tal, st)
                for b in range(4):
                    for kt in range(KT):
                        split_lo(w_part(b, 1)[:, kt], w_part(b, 0)[:, kt], xs, "w_hi", w_hi, w_lo)
                if st.bias == "mask":
                    for qt in range(NT):
                        i = tal["side"].next()
                        dve.wait_ge(side_full[qt], tal["side"].done(i))
                        nc.vector.tensor_scalar(FB[:, qt], FB[:, qt].bitcast(I32), 0.0, -FILL, ALU.is_equal,
                                                ALU.mult).then_inc(conv_done, 1)
                    dve.wait_ge(conv_done, NT)
                    gate()

                def largest(k):
                    n = tal["s"].next()
                    if st.bias == "side" and k < NT:
                        i = tal["side_ready"].marked(k)
                        dve.wait_ge(side_ready, tal["side_ready"].done(i))
                    dve.wait_ge(s_full, tal["s"].done(n))
                    if st.bias:
                        gate()
                        nc.vector.tensor_tensor_reduce(
                            out=PR[:, k % 4], in0=psS[:, n % 2], in1=FB[:, k % NT], scale=-st.scale, scalar=BIG,
                            op0=ALU.add, op1=ALU.min, accum_out=MN[:, k % 8:k % 8 + 1]).then_inc(s_evac, 1)
                    else:
                        nc.vector.tensor_scalar(PR[:, k % 4], psS[:, n % 2], -st.scale, None, ALU.mult, ALU.min,
                                                accum_out=MN[:, k % 8:k % 8 + 1]).then_inc(s_evac, 1)

                def projection_lo(name):
                    n = tal["j"].next()
                    tal["j_own"].next()
                    i = tal["j_hi"].next()
                    kind, g = name[0], name[1]
                    dve.wait_ge(j_hi, tal["j_hi"].done(i))
                    if kind in "QK":
                        col, qk = bias_col(st, kind, g), 2 * "QK".index(kind)
                        nc.vector.scalar_tensor_tensor(
                            out=QK[:, g % 2, qk + 1], in0=psJ[:, n % 2], scalar=COLS[:, col:col + 1], in1=f32(QK[:, g % 2, qk]),
                            op0=ALU.add, op1=ALU.subtract).then_inc(j_evac, 1)
                    else:
                        nc.vector.tensor_tensor(value_part(st, name, 1), projected(st, n), f32(value_part(st, name, 0)),
                                                ALU.subtract).then_inc(j_evac, 1)

                def head_sum(h):
                    j = h % st.per_group
                    n = tal["pv_half"].next()
                    og = OG[j * dk:(j + 1) * dk, :]
                    dve.wait_ge(pv_half, tal["pv_half"].done(n))
                    nc.vector.tensor_tensor(og, psV[0:dk, n % 2], og, ALU.add).then_inc(pv_evac, 1)

                def group_lo(g):
                    i = tal["o_hi"].next()
                    col = bias_col(st, "V", g)
                    dve.wait_ge(o_hi, tal["o_hi"].done(i))
                    nc.vector.scalar_tensor_tensor(
                        out=OT[:, 1, g], in0=OG[:, :], scalar=COLS[:, col:col + 1], in1=f32(OT[:, 0, g]),
                        op0=ALU.add, op1=ALU.subtract).then_inc(o_lo, 1)

                def out_sum(tt):
                    n = tal["j"].next()
                    own = tal["j_own"].next()
                    tal["j_own"].mark(tt)
                    i = tal["y"].next()
                    dve.wait_ge(j_full, tal["j"].done(n))
                    if st.cols != "ZERO":
                        m = tal["res"].next()
                        dve.wait_ge(res_ready, tal["res"].done(m))
                    else:
                        dve.wait_ge(y_full[tt], tal["y"].done(i))
                    nc.vector.tensor_tensor(Y[:, tt], psJ[:, n % 2], Y[:, tt], ALU.add).then_inc(j_evac, 1)
                    if st.norm:
                        stats(tt, j_evac, tal["j_own"].done(own))

                def run(steps, batch):
                    for step, k, _ in steps:
                        if step == "P_LO":
                            h, qt = divmod(k, NT)
                            n = tal["t"].next()
                            i = tal["t_hi"].next()
                            dve.wait_ge(t_hi, tal["t_hi"].done(i))
                            hi, lo = (PT[h % 2][:, p, :, qt * P:(qt + 1) * P] for p in range(2))
                            nc.vector.tensor_tensor(lo, psT[:, n % 2].rearrange("p (k t) -> p k t", k=NT), f32(hi),
                                                    ALU.subtract).then_inc(t_evac, 1)
                        elif step == "X_LO":
                            x_lo_part(k)
                        elif step == "PROB":
                            n = tal["exp"].next()
                            dve.wait_ge(exp_done, tal["exp"].done(n))
                            nc.vector.reciprocal(RS[:, k % 8:k % 8 + 1], SM[:, k % 8:k % 8 + 1]).then_inc(recip_done, 1)
                        elif step == "SIDE":
                            i = tal["side"].next()
                            tal["side_ready"].next()
                            tal["side_ready"].mark(k)
                            dve.wait_ge(side_full[k], tal["side"].done(i))
                            if k == 0:
                                dve.wait_ge(mask_ready, tal["mask_ready"].done(tal["mask_ready"].n - 1))
                            nc.vector.scalar_tensor_tensor(out=FB[:, k], in0=FB[:, k], scalar=1.0 / st.scale, in1=ROWS[:, 0],
                                                           op0=ALU.mult, op1=ALU.add).then_inc(side_ready, 1)
                        elif step == "MAX":
                            largest(k)
                        elif step == "HEAD_SUM":
                            head_sum(k)
                        elif step == "GROUP_LO":
                            group_lo(k)
                        elif step == "J_LO":
                            projection_lo(k)
                        elif step == "C_LO":
                            split_lo(cT[:, 1, k], cT[:, 0, k], cs, "cs_hi", cs_hi, cs_lo)
                        elif step == "OUT_SUM":
                            out_sum(k)
                        elif step == "NORM":
                            if st.norm:
                                normalise(k)
                            else:
                                dve.wait_ge(j_evac, tal["j_own"].done(tal["j_own"].marked(k)))
                                dve.sem_inc(y_norm, 1)
                        elif step == "ROWMASK":
                            i = tal["mask"].next()
                            tal["mask_ready"].next()
                            dve.wait_ge(mask_full, tal["mask"].done(i))
                            nc.vector.tensor_scalar(ROWS[:, 0], ROWS[:, 0].bitcast(I32), 0.0, -FILL, ALU.is_equal,
                                                    ALU.mult).then_inc(mask_ready, 1)

                stage_loop(dve, tal, st, ["x_hi", "s", "exp", "t_hi", "t", "pv_half", "o_hi", "j", "j_hi", "j_own", "y"],
                           run)

            tal.update(h=Tally(h_full, credit=2), used=Tally(h_used, credit=4), hi=Tally(h_hi))
            acc = [psJ[:, 0], psJ[:, 1], psV[:, 0], psV[:, 1]]
            for b in range(8):
                for kt in range(KT):
                    split_lo(w_part(b, 1)[:, kt], w_part(b, 0)[:, kt], xs, "w_hi", w_hi, w_lo)

            def hidden(f):
                n = tal["h"].next()
                i = tal["used"].next()
                m = tal["hi"].next()
                dve.wait_ge(h_full, tal["h"].done(n))
                dve.wait_ge(h_used, tal["used"].done(i - 4))
                nc.vector.tensor_copy(HH[:, n % 4], HF[:, n % 4]).then_inc(h_hi, 1)
                dve.wait_ge(h_hi, tal["hi"].done(m))
                nc.vector.tensor_tensor(HL[:, n % 4], HF[:, n % 4], f32(HH[:, n % 4]), ALU.subtract).then_inc(h_lo, 1)

            def results():
                dve.wait_ge(h_used, tal["used"].done(tal["used"].n - 1))
                own = []
                for tt in range(NT):
                    m = tal["res"].next()
                    own.append(tal["acc_own"].next())
                    dve.wait_ge(res_ready, tal["res"].done(m))
                    nc.vector.tensor_tensor(Y[:, tt], acc[tt], Y[:, tt], ALU.add).then_inc(acc_evac, 1)
                for tt in range(NT):
                    stats(tt, acc_evac, tal["acc_own"].done(own[tt]))
                for tt in range(NT):
                    normalise(tt)

            for tt in range(NT):
                x_lo_part(tt)
            per = dict(x_hi=NT, t=NT, h=NF, used=NF, hi=NF, res=NT, acc_own=NT, rstd=NT, y_sum=NT)
            with turns(dve, B - 1, [(tal[k], per[k]) for k in per]):
                for f in range(NF):
                    hidden(f)
                for tt in range(NT):
                    x_lo_part(tt)
                results()
            for f in range(NF):
                hidden(f)
            results()

        @block.gpsimd
        def _(pool):
            tal = dict(recip=Tally(recip_done), y=RingTally(y_full), mv=Tally(mv_ready), var=Tally(var_eps),
                       y_norm=Tally(y_norm), gain=Tally(y_gain))
            nc.gpsimd.memset(ID[:, :], 0.0).then_inc(ident_zero, 1)
            pool.wait_ge(ident_zero, 1)
            nc.gpsimd.affine_select(out=ID[:, :], in_=ID[:, :], compare_op=ALU.not_equal, fill=1.0, base=0,
                                    pattern=[[-1, P]], channel_multiplier=1).then_inc(ident_ready, 1)
            pool.wait_ge(const_ready, CONSTS)

            def gate():
                pool.sem_inc(gate_pool, 1)

            def residual(tt):
                i = tal["y"].next()
                pool.wait_ge(y_full[tt], tal["y"].done(i))
                nc.gpsimd.tensor_tensor(Y[:, tt], Y[:, tt], ROWS[:, 0], ALU.add).then_inc(res_ready, 1)

            def deviation(tt, eps):
                n = tal["mv"].next()
                i = tal["var"].next()
                pool.wait_ge(mv_ready, tal["mv"].done(n))
                nc.gpsimd.tensor_tensor(VE[:, tt:tt + 1], MV[:, tt, 1:2], CONST[:, EPS[eps]:EPS[eps] + 1],
                                        ALU.add).then_inc(var_eps, 1)
                pool.wait_ge(var_eps, tal["var"].done(i))
                nc.gpsimd.tensor_tensor(RD[:, tt:tt + 1], VE[:, tt:tt + 1], CONST[:, 0:1], ALU.pow).then_inc(rstd, 1)

            def gain_offset(tt):
                n = tal["y_norm"].next()
                i = tal["gain"].next()
                pool.wait_ge(y_norm, tal["y_norm"].done(n))
                nc.gpsimd.tensor_tensor(Y[:, tt], Y[:, tt], ROWS[:, 1], ALU.mult).then_inc(y_gain, 1)
                pool.wait_ge(y_gain, tal["gain"].done(i))
                nc.gpsimd.tensor_tensor(Y[:, tt], Y[:, tt], ROWS[:, 2], ALU.add).then_inc(y_done, 1)

            rows_seen = 16
            for st in STAGES:
                new_stage(tal, st)
                if st.rows:
                    rows_seen += 16 * (3 if st.cols != "ZERO" else 2)
                    pool.wait_ge(rows_full, rows_seen)

                def run(steps, batch):
                    for step, k, _ in steps:
                        if step == "PROB":
                            n = tal["recip"].next()
                            pool.wait_ge(recip_done, tal["recip"].done(n))
                            gate()
                            nc.gpsimd.tensor_scalar(PR[:, k % 4], PR[:, k % 4], RS[:, k % 8:k % 8 + 1], 1.0, ALU.mult,
                                                    ALU.mult).then_inc(p_ready, 1)
                        elif step == "RES" and st.cols != "ZERO":
                            residual(k)
                        elif step == "OUT_SUM" and st.norm:
                            deviation(k, st.eps)
                        elif step == "NORM" and st.norm:
                            gain_offset(k)

                stage_loop(pool, tal, st, ["recip"] + (["y_norm"] if st.norm else []) +
                           (["y"] if st.cols != "ZERO" else []), run)
                if not st.norm:
                    tal["y_norm"].n += B * NT
                if st.cols == "ZERO":
                    tal["y"].n += B * NT

            rows_seen += 48
            pool.wait_ge(rows_full, rows_seen)
            with turns(pool, B, [(tal[k], NT) for k in ("y", "mv", "var", "y_norm", "gain")]):
                for tt in range(NT):
                    residual(tt)
                for tt in range(NT):
                    deviation(tt, FF_EPS)
                for tt in range(NT):
                    gain_offset(tt)


def kernel(**inputs):
    import numpy as np
    import concourse.bacc as bacc
    from concourse import mybir
    from concourse.bass_utils import run_bass_kernel_spmd

    a = {k: np.asarray(v) for k, v in inputs.items()}
    h = AD
    l0 = lambda k: a["L0_xattn_" + k]
    l1 = lambda k: a["L1_xattn_" + k]
    blocks = []
    for half in range(2):
        cut = slice(half * h, (half + 1) * h)
        blocks += [l0("w_q")[:, cut], l0("w_k")[:, cut], l0("w_v")[:, cut], l0("w_o")[cut, :]]
    for p in ("sa", "ca"):
        blocks += [l1(f"{p}_w{m}").T for m in "qkvo"]
    blocks += [l1("ff_w1")[i * 512:(i + 1) * 512, :].T for i in range(FF // 512)]
    blocks += [l1("ff_w2")[:, i * 512:(i + 1) * 512].T for i in range(FF // 512)]
    columns = lambda v: v.reshape(-1, P).T
    arrays = {
        "x": a["x"],
        "ctx_t": a["ctx_1024"].transpose(0, 2, 1),
        "side": a["fside_Bx1xSxS2_0"],
        "key_mask": a["mask_Bx1x1xS2_ik0"].reshape(B, 1, 1, S),
        "pair_mask": a["mask_1x1xSxS_ik0"],
        "w": np.stack(blocks),
        "rows": np.stack([
            np.stack([l0("ln_b"), l0("ln_g"), l0("ln_b")]),
            np.stack([l1("sa_bo"), l1("ln1_g"), l1("ln1_b")]),
            np.stack([l1("ca_bo"), l1("ln2_g"), l1("ln2_b")]),
            np.stack([l1("ff_b2"), l1("ln3_g"), l1("ln3_b")])]),
        "cols": np.concatenate([columns(l1(f"{p}_b{m}")) for p in ("sa", "ca") for m in "qkv"]
                               + [columns(l1("ff_b1"))], axis=1),
    }
    nc = bacc.Bacc("TRN2", target_bir_lowering=False, num_devices=1, dynamic_dma_scratch_size=1024)
    feed, aps = {}, []
    for name, v in arrays.items():
        v = np.ascontiguousarray(v)
        feed[f"in_{name}"] = v
        aps.append(nc.dram_tensor(f"in_{name}", v.shape, mybir.dt.from_np(v.dtype), kind="ExternalInput").ap())
    out = nc.dram_tensor("result", (B, S, D), mybir.dt.float32, kind="ExternalOutput").ap()
    build(nc, *aps, out)
    r = run_bass_kernel_spmd(nc, [feed], core_ids=[0])
    return r.results[0]["result"]
```

```python
from contextlib import ExitStack, contextmanager

B, S, D, FF = 8, 512, 512, 2048
P = 128
NT = S // P
KT = D // P
NF = FF // P
AD = 512
NG = AD // P

COL = {"SA": 0, "CA": 12, "FF": 24, "ZERO": 40}
NCOL = 40
CONSTS = 4
ROW = {"L0": 0, "SA": 1, "CA": 2, "FF": 3}


class Stage:

    def __init__(self, name, dk, block, src, res, dst, context, bias, norm, eps, rows, cols):
        self.name, self.dk, self.block = name, dk, block
        self.src, self.res, self.dst = src, res, dst
        self.context, self.bias, self.norm, self.eps = context, bias, norm, eps
        self.rows, self.cols = rows, cols
        self.heads = AD // dk
        self.per_group = P // dk
        self.steps = self.heads * NT
        self.scale = float(dk) ** -0.5


STAGES = [
    Stage("L0a", 64, 0, "x", "x", "half", True, "side", False, 0.0, None, "ZERO"),
    Stage("L0b", 64, 4, "x", "half", "x1", True, "side", True, 1e-6, "L0", "ZERO"),
    Stage("SA", 32, 8, "x1", "x1", "x2", False, "mask", True, 1e-5, "SA", "SA"),
    Stage("CA", 32, 12, "x2", "x2", "x3", True, None, True, 1e-5, "CA", "CA"),
]
FF_BLOCK, FF_EPS = 16, 1e-5


STEPS = [
    "PROB",
    "P_LO",
    "X_LO",
    "HEAD_SUM",
    "J_LO",
    "OUT_SUM",
    "P_HI",
    "EXP",
    "SCORE",
    "X_TURN",
    "SIDE",
    "MAX",
    "PV",
    "HEAD_LO",
    "X_HI",
    "GROUP_HI",
    "GROUP_LO",
    "J_HI",
    "C_HI",
    "C_LO",
    "STACK",
    "RES",
    "STATS",
    "VAR",
    "NORM",
    "ROWMASK",
    "JOB",
    "TURN",
    "LOAD_X", "LOAD_C", "LOAD_MASK", "LOAD_SIDE", "LOAD_RES",
    "STORE",
]


def timetable(st):
    T, NH = st.steps, st.heads
    wide = st.dk == 64
    ev = []

    def add(slot, step, what=0):
        ev.append((slot, step, what))

    def job(name, slots, later=0):
        for part, slot in enumerate(slots):
            add(slot, "JOB", (name, part))
        if name[0] != "OUT":
            add(slots[-1] + 1 + later, "J_HI", name)
            add(slots[-1] + 2 + later, "J_LO", name)

    for s in range(T):
        add(s, "SCORE", s)
        add(s, "MAX", s)
        add(s + 1, "EXP", s)
        add(s + 2, "PROB", s)
        add(s + 3, "TURN", s)
        add(s + 4, "P_HI", s)
        add(s + 5, "P_LO", s)
    for h in range(NH):
        for kt in range(NT):
            add(NT * h + (9, 9, 10, 10)[kt], "PV", (h, kt))
        add(NT * h + 11, "HEAD_LO", h)
        add(NT * h + 12, "HEAD_SUM", h)
        if h % st.per_group == st.per_group - 1:
            add(NT * h + 13, "GROUP_HI", h // st.per_group)
            add(NT * h + 14, "GROUP_LO", h // st.per_group)
        for piece in range(3):
            first = (-4, -3, -2) if wide else (-3, -2, -2)
            add(NT * h + (first[piece] if h % st.per_group == 0 else piece - 5), "STACK", (h, piece))
    span = T // NG
    for g in range(NG):
        at = span * (g - 1) + (0 if wide else 8)
        job(("Q", g), [at, at, at + 1, at + 1])
        k_at = at + (1 if wide else 2)
        job(("K", g), [k_at, k_at, k_at + 1, k_at + 1])
    if wide:
        job(("V", 0, 0), [-4, -4, -3, -3])
        job(("V", 0, 1), [-2, -2, -1, -1])
        job(("V", 1, 0), [4, 4, 5, 5], 1)
        job(("V", 1, 1), [6, 6, 7, 7])
    else:
        job(("V", 0, 0), [0, 1, 2, 3])
        job(("V", 0, 1), [4, 5, 6, 7])
        job(("V", 1, 0), [28, 29, 30, 31])
        job(("V", 1, 1), [32, 33, 34, 35])
    for tt in range(NT):
        x_at = -12 + tt if wide else -18 + tt + 2 * (tt // 2)
        add(x_at, "X_TURN", tt)
        add(x_at, "X_HI", tt)
        add(x_at + 1, "X_LO", tt)
        add(x_at - 6 if tt < 2 else x_at - (1 if wide else 3), "LOAD_X", tt)
        if st.context:
            c_at = x_at + (tt // 2 if wide else 1)
            add(c_at, "C_HI", tt)
            add(c_at + 1, "C_LO", tt)
            add(c_at - 7 if tt < 2 else c_at - 2, "LOAD_C", tt)
        step = 1 if wide else 2
        out = T + (11 + tt if wide else 12 + 3 * tt)
        job(("OUT", tt), [out] * 4 if wide else [out, out, out + 1, out + 1])
        add(T + 4 + tt, "LOAD_RES", tt)
        add(T + 8 + tt, "RES", tt)
        add(out + step, "OUT_SUM", tt)
        if st.norm:
            add(out + step + 1, "STATS", tt)
            add(out + step + 2, "VAR", tt)
        add(out + step + (4 if wide else 5), "NORM", tt)
        add(out + step + (5 if wide else 6), "STORE", tt)
        if st.bias == "side":
            add(tt - 4, "LOAD_SIDE", tt)
            add(tt - 1, "SIDE", tt)
    if st.bias == "side":
        add(-10, "LOAD_MASK")
        add(-6, "ROWMASK")
    return sorted(ev, key=lambda e: (e[0], STEPS.index(e[1])))


def body_steps(st, prev, nxt):
    T = st.steps
    ev = []
    for slot, step, what in timetable(st):
        off = -1 if slot >= T else 1 if slot < 0 else 0
        if off == 0 or (prev if off < 0 else nxt):
            ev.append((slot % T, STEPS.index(step), step, what, off))
    return [e[2:] for e in sorted(ev, key=lambda e: (e[0], e[1], e[4]))]


def prologue(st):
    return [(step, what, 0) for slot, step, what in timetable(st) if slot < 0]


def drain(st):
    return [(step, what, 0) for slot, step, what in timetable(st) if slot >= st.steps]


class Tally:

    def __init__(self, sem, unit=1, credit=0):
        self.sem, self.unit, self.credit = sem, unit, credit
        self.n, self.per, self.turn, self.marks = 0, 0, None, {}

    def next(self):
        self.n += 1
        return self.n - 1

    def mark(self, name):
        self.marks[name] = self.n - 1

    def marked(self, name):
        return self.marks.get(name)

    def done(self, n):
        v = self.unit * (n + 1) + self.credit
        return v if self.turn is None else self.turn * (self.per * self.unit) + v


class RingTally(Tally):

    def __init__(self, sems, unit=16, credit=0):
        Tally.__init__(self, None, unit, credit)
        self.sems = sems

    def slot(self, n):
        return n % len(self.sems)

    def sem_of(self, n):
        return self.sems[n % len(self.sems)]

    def done(self, n):
        R = len(self.sems)
        v = self.unit * (n // R + 1) + self.credit
        return v if self.turn is None else self.turn * (self.per // R * self.unit) + v


@contextmanager
def turns(eng, count, tallies):
    first = [t.n for t, _ in tallies]
    with eng.Fori(0, count) as r:
        for t, per in tallies:
            t.per, t.turn = per, r
        yield r
    for (t, per), n in zip(tallies, first):
        assert t.n - n == per, (t.sem, t.n - n, per)
        t.turn = None
        t.n += per * (count - 1)
        t.marks = {k: v + per * (count - 1) for k, v in t.marks.items()}


def build(nc, x, ctx_t, side, key_mask, pair_mask, w, rows, cols, out):
    import concourse.bass as bass
    from concourse import mybir

    F32, F32R, I32 = mybir.dt.float32, mybir.dt.float32r, mybir.dt.int32
    ALU, ACT = mybir.AluOpType, mybir.ActivationFunctionType
    BIG = 3.0e38
    FILL = 1.0e30

    dram = {"x": x, "out": out}
    for name in ("half", "x1", "x2", "x3"):
        dram[name] = nc.dram_tensor(name, (B, S, D), F32, kind="Internal").ap()

    with ExitStack() as stack:
        def sb(name, shape, dt=F32):
            return stack.enter_context(nc.sbuf_tensor(name, shape, dt))

        def sem(name):
            return stack.enter_context(nc.semaphore(name))

        W = sb("W", [P, 8, KT, D], F32R)
        R = sb("R", [P, 8, KT, D], F32R)
        cT = R[:, 0:2]
        VAL = R[:, 2:4].rearrange("p a k n -> p (a k n)").rearrange("p (k n) -> p k n", k=NT)
        PT = [R[:, 4 + 2 * i:6 + 2 * i] for i in range(2)]
        xT = sb("xT", [P, 2, KT, S], F32R)
        RAW = sb("RAW", [P, 8, D])
        xs, cs = RAW[:, 0:2], RAW[:, 2:4]
        FB = RAW[:, 4:8]
        QK = sb("QK", [P, 4, S], F32R)
        QS = sb("QS", [P, 2, 3, S], F32R)
        PR = sb("PR", [P, 4, S])
        OT = sb("OT", [P, 2, NG, S], F32R)
        OG = sb("OG", [P, S])
        Y = sb("Y", [P, NT, D])
        ROWS = sb("ROWS", [P, 3, D])
        COLS = sb("COLS", [P, NCOL + NG])
        MN = sb("MN", [P, 8])
        SM = sb("SM", [P, 8])
        RS = sb("RS", [P, 8])
        ID = sb("ID", [P, P])
        ST = sb("ST", [P, NT, 6])
        MV = sb("MV", [P, NT, 2])
        VE = sb("VE", [P, NT])
        RD = sb("RD", [P, NT])
        CONST = sb("CONST", [P, 3])
        EPS = {1e-6: 1, 1e-5: 2}
        HF = PR
        HH, HL = QK[:, :], QS.rearrange("p r c n -> p (r c) n")[:, 0:4]

        psS = stack.enter_context(nc.psum_tensor("psS", [P, 2, 512], F32))
        psT = stack.enter_context(nc.psum_tensor("psT", [P, 3, 512], F32))
        psJ = stack.enter_context(nc.psum_tensor("psJ", [P, 2, 512], F32))
        psV = stack.enter_context(nc.psum_tensor("psV", [P, 512], F32))

        xs_full = [sem(f"xs_full{i}") for i in range(2)]
        ws_full = [sem(f"ws_full{i}") for i in range(8)]
        cs_full = [sem(f"cs_full{i}") for i in range(2)]
        side_full = [sem(f"side_full{i}") for i in range(NT)]
        mask_full = sem("mask_full")
        rows_full = sem("rows_full")
        y_full = [sem(f"y_full{i}") for i in range(NT)]
        y_stored = [sem(f"y_stored{i}") for i in range(NT)]
        const_ready = sem("const_ready")
        ident_ready = sem("ident_ready")
        ident_zero = sem("ident_zero")
        x_hi = sem("x_hi")
        w_hi = sem("w_hi")
        w_lo = sem("w_lo")
        cs_hi = sem("cs_hi")
        cs_lo = sem("cs_lo")
        s_full = sem("s_full")
        s_evac = sem("s_evac")
        exp_done = sem("exp_done")
        recip_done = sem("recip_done")
        p_ready = sem("p_ready")
        stacked = sem("stacked")
        t_full = sem("t_full")
        t_hi = sem("t_hi")
        t_evac = sem("t_evac")
        pv_full = sem("pv_full")
        pv_half = sem("pv_half")
        pv_evac = sem("pv_evac")
        o_hi = sem("o_hi")
        o_lo = sem("o_lo")
        j_full = sem("j_full")
        j_hi = sem("j_hi")
        j_evac = sem("j_evac")
        mask_ready = sem("mask_ready")
        side_ready = sem("side_ready")
        res_ready = sem("res_ready")
        mv_ready = sem("mv_ready")
        var_eps = sem("var_eps")
        rstd = sem("rstd")
        y_norm = sem("y_norm")
        y_gain = sem("y_gain")
        y_done = sem("y_done")
        y_sum = sem("y_sum")
        conv_done = sem("conv_done")
        u_full = sem("u_full")
        h_full = sem("h_full")
        h_hi = sem("h_hi")
        h_lo = sem("h_lo")
        h_used = sem("h_used")
        acc_evac = sem("acc_evac")
        gate_dve = sem("gate_dve")
        gate_pool = sem("gate_pool")

        def w_part(b, part):
            return (W if b < 4 else R)[:, 2 * (b % 4) + part]

        def f32(ap):
            return ap.bitcast(F32)

        def counts(st):
            T, H = st.steps, st.heads
            return dict(xs=NT, x_hi=NT, cs=KT, cs_hi=KT, cs_lo=KT, s=T, s_full=T, exp=T, recip=T, p=T, t=T, t_hi=T,
                        pv=H, pv_half=H, pv_evac=H, o_hi=NG, o_lo=NG, j=2 * NG + 3 * NT, j_own=2 * NG + 3 * NT,
                        j_hi=2 * NG + NT, stack=H, pieces=3 * H, mask=1, mask_ready=1, side=NT, side_ready=NT, res=NT, y=NT, mv=NT,
                        var=NT, rstd=NT, y_norm=NT, gain=NT, y_done=NT, y_sum=NT)

        def turned(st, k):
            return psT[:, 1 if k == st.steps - 1 else k % 3]

        def bias_col(st, which, g):
            return COL[st.cols] + (0 if st.cols == "ZERO" else "QKV".index(which) * NG) + g

        def value_part(st, name, part):
            half, pair, n = name[1], name[2], st.heads // 2
            v = VAL[:, 2 * pair:2 * pair + 2].rearrange("p t (h c) -> p t h c", c=2 * st.dk)
            return v[:, :, half * n:(half + 1) * n, part * st.dk:(part + 1) * st.dk]

        def projected(st, n):
            return psJ[:, n % 2].rearrange("p (t h c) -> p t h c", t=2, c=st.dk)

        def new_stage(tal, st):
            for t in tal.values():
                t.marks.clear()

        def stage_loop(eng, tal, st, names, run, before_drain=lambda st: None):
            per = counts(st)
            names = names + (["cs", "cs_hi", "cs_lo"] if st.context else [])
            names = names + (["mask", "mask_ready", "side", "side_ready"] if st.bias == "side" else [])
            names = names + (["mv", "var", "rstd", "gain", "y_sum", "y_done"] if st.norm else [])
            names = names + (["res"] if st.cols != "ZERO" else [])
            run(prologue(st), 0)
            run(body_steps(st, False, True), 0)
            with turns(eng, B - 2, [(tal[k], per[k]) for k in dict.fromkeys(names) if k in tal]) as r:
                run(body_steps(st, True, True), r + 1)
            run(body_steps(st, True, False), B - 1)
            before_drain(st)
            run(drain(st), B - 1)

        block = stack.enter_context(nc.Block())

        @block.sync
        def _(sp):
            tal = dict(xs=RingTally(xs_full), x_hi=Tally(x_hi, credit=2), cs=RingTally(cs_full),
                       cs_lo=Tally(cs_lo, credit=2), ws=RingTally(ws_full), w_lo=Tally(w_lo, credit=8),
                       s=Tally(s_evac, credit=2), side=RingTally(side_full), side_ready=Tally(side_ready),
                       y=RingTally(y_stored, credit=16), y_norm=Tally(y_norm), y_done=Tally(y_done))
            for tt in range(NT):
                sp.sem_inc(y_stored[tt], 16)
            sp.dma_start(COLS[:, 0:NCOL], cols).then_inc(rows_full, 16)

            def load_x(src, b, tt):
                n = tal["x_hi"].next()
                sp.wait_ge(x_hi, tal["x_hi"].done(n - 2))
                i = tal["xs"].next()
                sp.dma_start(xs[:, tal["xs"].slot(i)], dram[src][b, tt * P:(tt + 1) * P, :]).then_inc(
                    tal["xs"].sem_of(i), 16)

            def load_w(src):
                n = tal["w_lo"].next()
                sp.wait_ge(w_lo, tal["w_lo"].done(n - 8))
                i = tal["ws"].next()
                sp.dma_start(RAW[:, tal["ws"].slot(i)], src).then_inc(tal["ws"].sem_of(i), 16)

            def load_c(st, b, tt):
                n = tal["cs_lo"].next()
                sp.wait_ge(cs_lo, tal["cs_lo"].done(n - 2))
                i = tal["cs"].next()
                sp.dma_start(cs[:, tal["cs"].slot(i)], ctx_t[b, tt * P:(tt + 1) * P, :]).then_inc(
                    tal["cs"].sem_of(i), 16)

            def load_res(res, b, tt):
                i = tal["y"].next()
                sp.wait_ge(y_stored[tt], tal["y"].done(i - NT))
                sp.dma_start(Y[:, tt], dram[res][b, tt * P:(tt + 1) * P, :]).then_inc(y_full[tt], 16)

            def store(name, norm, b, tt):
                which, ready = ("y_done", y_done) if norm else ("y_norm", y_norm)
                n = tal[which].next()
                sp.wait_ge(ready, tal[which].done(n))
                sp.dma_start(dram[name][b, tt * P:(tt + 1) * P, :], Y[:, tt]).then_inc(y_stored[tt], 16)

            def tiles(first, count):
                return [w[first + b, kt * P:(kt + 1) * P, :] for b in range(count) for kt in range(KT)]

            def ahead(st):
                sp.wait_ge(x_hi, tal["x_hi"].done(tal["x_hi"].n - 1))
                if st.context:
                    sp.wait_ge(cs_lo, tal["cs_lo"].done(tal["cs_lo"].n - 1))
                sp.wait_ge(s_evac, tal["s"].done(tal["s"].n - 1))
                for tile in tiles(st.block + 4, 4)[:len(ws_full)]:
                    load_w(tile)

            def begin(rows, bias_row, weight_tiles):
                for tile in weight_tiles[len(ws_full) if tal["y"].n else 0:]:
                    load_w(tile)
                if tal["y"].n:
                    for tt in range(NT):
                        sp.wait_ge(y_stored[tt], tal["y"].done(tal["y"].n - NT + tt))
                if rows is not None:
                    for k in range(0 if bias_row else 1, 3):
                        sp.dma_start(ROWS[:, k], rows_d(rows, k)).then_inc(rows_full, 16)
                sp.wait_ge(w_lo, tal["w_lo"].done(tal["w_lo"].n - 1))

            def rows_d(name, k):
                return rows[ROW[name], k:k + 1, :].to_broadcast([P, D])

            for st in STAGES:
                new_stage(tal, st)
                begin(st.rows, st.cols != "ZERO", tiles(st.block, 4))
                if st.bias == "mask":
                    for qt in range(NT):
                        i = tal["side"].next()
                        sp.dma_start(FB[:, qt].bitcast(I32), pair_mask[0, 0, qt * P:(qt + 1) * P, :]).then_inc(
                            tal["side"].sem_of(i), 16)

                def run(steps, batch):
                    for step, k, off in steps:
                        b = batch + off
                        if step == "MAX":
                            tal["s"].next()
                            tal["s"].mark(k)
                        elif step == "SIDE":
                            tal["side_ready"].next()
                            tal["side_ready"].mark(k)
                        elif step == "LOAD_X":
                            load_x(st.src, b, k)
                        elif step == "LOAD_C":
                            load_c(st, b, k)
                        elif step == "LOAD_MASK":
                            last = tal["side_ready"].marked(NT - 1)
                            if last is not None:
                                sp.wait_ge(side_ready, tal["side_ready"].done(last))
                            sp.dma_start(ROWS[:, 0].bitcast(I32), key_mask[b, 0, 0:1, :].to_broadcast([P, S])).then_inc(
                                mask_full, 16)
                        elif step == "LOAD_SIDE":
                            i = tal["side"].next()
                            last = tal["s"].marked(st.steps - NT + k)
                            if last is not None:
                                sp.wait_ge(s_evac, tal["s"].done(last))
                            sp.dma_start(FB[:, k], side[b, 0, k * P:(k + 1) * P, :]).then_inc(tal["side"].sem_of(i), 16)
                        elif step == "LOAD_RES":
                            load_res(st.res, b, k)
                        elif step == "STORE":
                            store(st.dst, st.norm, b, k)

                stage_loop(sp, tal, st, ["xs", "x_hi", "s", "y"] +
                           ([] if st.norm else ["y_norm"]), run, ahead)
                if st.norm:
                    tal["y_norm"].n += B * NT

            begin("FF", True, tiles(FF_BLOCK, 8))

            def ff_inputs(b):
                for tt in range(NT):
                    load_x("x3", b, tt)

            def ff_residuals(b):
                for tt in range(NT):
                    load_res("x3", b, tt)

            def ff_stores(b):
                for tt in range(NT):
                    store("out", True, b, tt)

            ff_inputs(0)
            ff_residuals(0)
            ff_inputs(1)
            with turns(sp, B - 2, [(tal[k], NT) for k in ("xs", "x_hi", "y", "y_done")]) as r:
                ff_stores(r)
                ff_residuals(r + 1)
                ff_inputs(r + 2)
            ff_stores(B - 2)
            ff_residuals(B - 1)
            ff_stores(B - 1)
            for tt in range(NT):
                sp.wait_ge(y_stored[tt], tal["y"].done(tal["y"].n - NT + tt))

        @block.tensor
        def _(pe):
            tal = dict(xs=RingTally(xs_full), w_lo=Tally(w_lo, credit=8), cs_lo=Tally(cs_lo, credit=2), s=Tally(s_evac, credit=2),
                       p=Tally(p_ready), t=Tally(t_evac, credit=2), pv=Tally(pv_evac, credit=1),
                       o_lo=Tally(o_lo, credit=1), j=Tally(j_evac, credit=2), stack=Tally(stacked, unit=3))
            pe.sem_inc(h_used, 4)
            pe.wait_ge(ident_ready, 1)

            def three(dst, a, b, first=True, last=True):
                nc.tensor.matmul(dst, a[0], b[0], start=first, stop=False)
                nc.tensor.matmul(dst, a[0], b[1], start=False, stop=False)
                return nc.tensor.matmul(dst, a[1], b[0], start=False, stop=last)

            def parts(t, kt, cols):
                return [t[:, p, kt, cols] for p in range(2)]

            def w_parts(b, kt, cols):
                return [w_part(b, p)[:, kt, cols] for p in range(2)]

            def x_turn(tt, psum=psT, ring="t", evac=t_evac, full=t_full):
                i = tal["xs"].next()
                n = tal[ring].next()
                pe.wait_ge(tal["xs"].sem_of(i), tal["xs"].done(i))
                pe.wait_ge(evac, tal[ring].done(n - 2))
                for kt in range(KT):
                    mm = nc.tensor.transpose(psum[:, n % 2, kt * P:(kt + 1) * P],
                                             xs[:, tal["xs"].slot(i), kt * P:(kt + 1) * P], ID[:, :])
                mm.then_inc(full, 1)

            def weights(count):
                for _ in range(count):
                    n = tal["w_lo"].next()
                pe.wait_ge(w_lo, tal["w_lo"].done(n))

            for st in STAGES:
                dk = st.dk
                src = cT if st.context else xT
                new_stage(tal, st)
                weights(4 * KT)

                def score(k):
                    h, qt = divmod(k, NT)
                    n = tal["s"].next()
                    if qt == 0:
                        i = tal["stack"].next()
                        pe.wait_ge(stacked, tal["stack"].done(i))
                    pe.wait_ge(s_evac, tal["s"].done(n - 2))
                    tile = slice(qt * P, (qt + 1) * P)
                    q, kk, k_lo = (QS[:, h % 2, c] for c in range(3))
                    if dk == 64:
                        nc.tensor.matmul(psS[:, n % 2], q[:, tile], kk, start=True, stop=False)
                        mm = nc.tensor.matmul(psS[:, n % 2], q[0:dk, tile], k_lo[0:dk], start=False, stop=True)
                    else:
                        mm = nc.tensor.matmul(psS[:, n % 2], q[0:3 * dk, tile], kk[0:3 * dk], start=True, stop=True)
                    mm.then_inc(s_full, 1)

                def turn(k):
                    n = tal["t"].next()
                    i = tal["p"].next()
                    pe.wait_ge(p_ready, tal["p"].done(i))
                    slot = 1 if k == st.steps - 1 else k % 3
                    last = tal["t"].marked(("slot", slot))
                    if last is not None:
                        pe.wait_ge(t_evac, tal["t"].done(last))
                    tal["t"].mark(("slot", slot))
                    for kt in range(NT):
                        mm = nc.tensor.transpose(turned(st, k)[:, kt * P:(kt + 1) * P], PR[:, k % 4, kt * P:(kt + 1) * P],
                                                 ID[:, :])
                    mm.then_inc(t_full, 1)
                    tal["t"].mark(("turned", k))

                def values(h, kt):
                    if kt == 0:
                        n = tal["pv"].next()
                        pe.wait_ge(t_evac, tal["t"].done(tal["t"].marked(("turned", NT * h + NT - 1))))
                        pe.wait_ge(pv_evac, tal["pv"].done(n - 1))
                    if h % (st.heads // 2) == 0 and kt % 2 == 0:
                        made = tal["j"].marked(("V", h // (st.heads // 2), kt // 2))
                        pe.wait_ge(j_evac, tal["j"].done(made))
                    for p in range(2):
                        mm = nc.tensor.matmul(psV[0:2 * dk], VAL[:, kt, 2 * dk * h:2 * dk * (h + 1)],
                                              PT[h % 2][:, p, kt, :], start=(kt == 0 and p == 0),
                                              stop=(kt == NT - 1 and p == 1))
                    if kt == NT - 1:
                        mm.then_inc(pv_full, 1)

                def job(name, part):
                    if part == 0:
                        n = tal["j"].next()
                        tal["j"].mark(name)
                        if name == ("Q", 0):
                            pe.wait_ge(j_evac, tal["j"].done(tal["j"].marked(("x", NT - 1))))
                        if name == ("K", 0) and st.context:
                            pe.wait_ge(cs_lo, tal["cs_lo"].done(tal["cs_lo"].marked(NT - 1)))
                        if name == ("OUT", 0):
                            pe.wait_ge(o_lo, tal["o_lo"].done(tal["o_lo"].marked(NG - 1)))
                        pe.wait_ge(j_evac, tal["j"].done(n - 2))
                    n = tal["j"].n - 1
                    kind, last = name[0], part == KT - 1
                    if kind in "QK":
                        cols = slice(name[1] * P, (name[1] + 1) * P)
                        data, b = (xT, 0) if kind == "Q" else (src, 1)
                        mm = three(psJ[:, n % 2], w_parts(b, part, cols), parts(data, part, slice(0, S)), part == 0, last)
                    elif kind == "OUT":
                        tile = slice(name[1] * P, (name[1] + 1) * P)
                        mm = three(psJ[:, n % 2], parts(OT, part, tile), w_parts(3, part, slice(0, D)), part == 0, last)
                    else:
                        half, which = AD // 2, part // 2
                        tile = slice((2 * name[2] + which) * P, (2 * name[2] + which + 1) * P)
                        for kt in (0, 1) if part % 2 == 0 else (2, 3):
                            mm = three(psJ[:, n % 2, which * half:(which + 1) * half], parts(src, kt, tile),
                                       w_parts(2, kt, slice(name[1] * half, (name[1] + 1) * half)), kt == 0, kt == KT - 1)
                    if last:
                        mm.then_inc(j_full, 1)

                def run(steps, batch):
                    for step, k, _ in steps:
                        if step == "SCORE":
                            score(k)
                        elif step == "TURN":
                            turn(k)
                        elif step == "X_TURN":
                            x_turn(k, psJ, "j", j_evac, j_full)
                            tal["j"].mark(("x", k))
                        elif step == "PV":
                            values(*k)
                        elif step == "JOB":
                            job(*k)
                        elif step == "C_LO":
                            tal["cs_lo"].next()
                            tal["cs_lo"].mark(k)
                        elif step == "GROUP_LO":
                            tal["o_lo"].next()
                            tal["o_lo"].mark(k)

                stage_loop(pe, tal, st, ["xs", "s", "p", "t", "pv", "o_lo", "j", "stack"], run)

            tal.update(u=Tally(h_full, credit=2), h=Tally(h_lo, credit=4), acc=Tally(acc_evac, credit=NT))
            weights(8 * KT)
            acc = [psJ[:, 0], psJ[:, 1], psV[:, :], psT[:, 2]]

            def up(f, x_last):
                n = tal["u"].next()
                if f == 0:
                    pe.wait_ge(t_evac, tal["t"].done(x_last))
                pe.wait_ge(h_full, tal["u"].done(n - 2))
                for kt in range(KT):
                    mm = three(psS[:, n % 2], w_parts(f // 4, kt, slice((f % 4) * P, (f % 4 + 1) * P)),
                               parts(xT, kt, slice(0, S)), kt == 0, kt == KT - 1)
                mm.then_inc(u_full, 1)

            def down(f):
                n = tal["h"].next()
                pe.wait_ge(h_lo, tal["h"].done(n))
                if f == 0:
                    for tt in range(NT):
                        i = tal["acc"].next()
                    pe.wait_ge(acc_evac, tal["acc"].done(i - NT))
                for tt in range(NT):
                    h = [t[:, n % 4, tt * P:(tt + 1) * P] for t in (HH, HL)]
                    mm = three(acc[tt], h, w_parts(4 + f // 4, f % 4, slice(0, D)), f == 0, f == NF - 1)
                mm.then_inc(h_used, 1)

            def ff(x_last, nxt):
                up(0, x_last)
                up(1, None)
                for f in range(2, NF):
                    up(f, None)
                    down(f - 2)
                for f in range(2):
                    if nxt:
                        x_turn(2 * f)
                        x_turn(2 * f + 1)
                    down(NF - 2 + f)

            for tt in range(NT):
                x_turn(tt)
            with turns(pe, B - 1, [(tal["xs"], NT), (tal["t"], NT), (tal["u"], NF), (tal["h"], NF), (tal["acc"], NT)]):
                ff(tal["t"].n - 1, True)
            ff(tal["t"].n - 1, False)

        @block.scalar
        def _(act):
            tal = dict(ws=RingTally(ws_full), cs=RingTally(cs_full), t=Tally(t_full), s=Tally(s_evac, credit=2), pv=Tally(pv_full),
                       o_lo=Tally(o_lo, credit=1), pv_evac=Tally(pv_evac, credit=1), j=Tally(j_full),
                       stack=Tally(stacked, unit=3))
            act.sem_inc(x_hi, 2)
            act.sem_inc(h_full, 2)
            act.wait_ge(const_ready, CONSTS)
            act.wait_ge(rows_full, 16)

            def split_hi(dst, src, which, done):
                i = tal[which].next()
                act.wait_ge(tal[which].sem_of(i), tal[which].done(i))
                nc.scalar.activation(dst, src[:, tal[which].slot(i)], ACT.Copy).then_inc(done, 1)

            def x_hi_part(tt, psum=psT, ring="t", full=t_full):
                n = tal[ring].next()
                act.wait_ge(full, tal[ring].done(n))
                nc.scalar.activation(xT[:, 0, :, tt * P:(tt + 1) * P],
                                     psum[:, n % 2].rearrange("p (k t) -> p k t", k=KT), ACT.Copy).then_inc(x_hi, 1)

            for st in STAGES:
                dk = st.dk
                last = tal["j"].marked(("OUT", NT - 1))
                new_stage(tal, st)
                for b in range(4):
                    if b == 3 and last is not None:
                        act.wait_ge(j_full, tal["j"].done(last))
                    for kt in range(KT):
                        split_hi(w_part(b, 0)[:, kt], RAW, "ws", w_hi)

                def projection_hi(name):
                    n = tal["j"].next()
                    tal["j"].mark(name)
                    kind, g = name[0], name[1]
                    used = tal["stack"].marked((g - 1) % NG * st.per_group + st.per_group - 1)
                    if kind == "Q" and used is not None:
                        act.wait_ge(stacked, tal["stack"].done(used))
                    act.wait_ge(j_full, tal["j"].done(n))
                    if kind in "QK":
                        col = bias_col(st, kind, g)
                        nc.scalar.activation(QK[:, 2 * "QK".index(kind)], psJ[:, n % 2], ACT.Identity,
                                             bias=COLS[:, col:col + 1]).then_inc(j_hi, 1)
                    else:
                        nc.scalar.activation(value_part(st, name, 0), projected(st, n), ACT.Copy).then_inc(j_hi, 1)

                def head_lo(h):
                    g, j = divmod(h, st.per_group)
                    n = tal["pv"].next()
                    act.wait_ge(pv_full, tal["pv"].done(n))
                    if j == 0:
                        i = tal["o_lo"].next()
                        act.wait_ge(o_lo, tal["o_lo"].done(i - 1))
                    nc.scalar.activation(OG[j * dk:(j + 1) * dk, :], psV[dk:2 * dk], ACT.Copy).then_inc(pv_half, 1)

                def group_hi(g):
                    last = tal["j"].marked(("OUT", NT - 1))
                    if g == 0 and last is not None:
                        act.wait_ge(j_full, tal["j"].done(last))
                    col = bias_col(st, "V", g)
                    act.wait_ge(pv_evac, tal["pv_evac"].done(tal["pv_evac"].n - 1))
                    nc.scalar.activation(OT[:, 0, g], OG[:, :], ACT.Identity, bias=COLS[:, col:col + 1]).then_inc(o_hi, 1)

                def run(steps, batch):
                    for step, k, _ in steps:
                        if step == "EXP":
                            n = tal["s"].next()
                            act.wait_ge(s_evac, tal["s"].done(n))
                            nc.scalar.activation(PR[:, k % 4], PR[:, k % 4], ACT.Exp, bias=MN[:, k % 8:k % 8 + 1], scale=-1.0,
                                                 accum_out=SM[:, k % 8:k % 8 + 1]).then_inc(exp_done, 1)
                        elif step == "P_HI":
                            h, qt = divmod(k, NT)
                            n = tal["t"].next()
                            act.wait_ge(t_full, tal["t"].done(n))
                            nc.scalar.activation(PT[h % 2][:, 0, :, qt * P:(qt + 1) * P],
                                                 turned(st, k).rearrange("p (k t) -> p k t", k=NT), ACT.Copy).then_inc(t_hi, 1)
                        elif step == "X_HI":
                            x_hi_part(k, psJ, "j", j_full)
                        elif step == "C_HI":
                            split_hi(cT[:, 0, k], cs, "cs", cs_hi)
                        elif step == "HEAD_LO":
                            head_lo(k)
                        elif step == "HEAD_SUM":
                            tal["pv_evac"].next()
                        elif step == "GROUP_HI":
                            group_hi(k)
                        elif step == "J_HI":
                            projection_hi(k)
                        elif step == "OUT_SUM":
                            tal["j"].next()
                            tal["j"].mark(("OUT", k))
                        elif step == "STACK" and k[1] == 2:
                            tal["stack"].next()
                            tal["stack"].mark(k[0])

                stage_loop(act, tal, st, ["t", "s", "pv", "o_lo", "pv_evac", "j", "stack"], run)

            tal.update(u=Tally(u_full), h=Tally(h_lo, credit=4))
            last = tal["j"].marked(("OUT", NT - 1))
            for b in range(8):
                if b == 3:
                    act.wait_ge(j_full, tal["j"].done(last))
                for kt in range(KT):
                    split_hi(w_part(b, 0)[:, kt], RAW, "ws", w_hi)

            def relu(f):
                n = tal["u"].next()
                i = tal["h"].next()
                act.wait_ge(u_full, tal["u"].done(n))
                act.wait_ge(h_lo, tal["h"].done(i - 4))
                nc.scalar.activation(HF[:, n % 4], psS[:, n % 2], ACT.Relu,
                                     bias=COLS[:, COL["FF"] + f:COL["FF"] + f + 1]).then_inc(h_full, 1)

            for tt in range(NT):
                x_hi_part(tt)
            with turns(act, B - 1, [(tal["t"], NT), (tal["u"], NF), (tal["h"], NF)]):
                for f in range(NF):
                    relu(f)
                for tt in range(NT):
                    x_hi_part(tt)
            for f in range(NF):
                relu(f)

        @block.vector
        def _(dve):
            tal = dict(x_hi=Tally(x_hi, credit=2), w_hi=Tally(w_hi), cs_hi=Tally(cs_hi), s=Tally(s_full), exp=Tally(exp_done),
                       t_hi=Tally(t_hi), t=Tally(t_full), pv_half=Tally(pv_half), pv=Tally(pv_full), o_hi=Tally(o_hi),
                       j=Tally(j_full), j_hi=Tally(j_hi), j_own=Tally(j_evac, credit=2),
                       acc_own=Tally(acc_evac, credit=NT), mask=Tally(mask_full, unit=16), side=RingTally(side_full),
                       side_ready=Tally(side_ready), y=RingTally(y_full), res=Tally(res_ready), rstd=Tally(rstd),
                       y_sum=Tally(y_sum), mask_ready=Tally(mask_ready), mv=Tally(mv_ready), gain=Tally(y_gain))
            nc.vector.memset(CONST[:, 0:1], -0.5).then_inc(const_ready, 1)
            nc.vector.memset(CONST[:, 1:2], 1e-6).then_inc(const_ready, 1)
            nc.vector.memset(CONST[:, 2:3], 1e-5).then_inc(const_ready, 1)
            nc.vector.memset(COLS[:, NCOL:NCOL + NG], 0.0).then_inc(const_ready, 1)
            dve.sem_inc(s_evac, 2)
            dve.sem_inc(t_evac, 2)
            dve.sem_inc(pv_evac, 1)
            dve.sem_inc(j_evac, 2)
            dve.sem_inc(o_lo, 1)
            dve.sem_inc(acc_evac, NT)
            dve.sem_inc(w_lo, 8)
            dve.sem_inc(cs_lo, 2)
            dve.sem_inc(h_lo, 4)

            def gate():
                dve.sem_inc(gate_dve, 1)

            def x_lo_part(tt, psum=psT, ring="t", evac=t_evac):
                n = tal[ring].next()
                i = tal["x_hi"].next()
                dve.wait_ge(x_hi, tal["x_hi"].done(i))
                hi, lo = (xT[:, p, :, tt * P:(tt + 1) * P] for p in range(2))
                nc.vector.tensor_tensor(lo, psum[:, n % 2].rearrange("p (k t) -> p k t", k=KT), f32(hi),
                                        ALU.subtract).then_inc(evac, 1)

            def split_lo(dst, hi, src, ring, which, split, done):
                n = tal[which].next()
                dve.wait_ge(split, tal[which].done(n))
                nc.vector.tensor_tensor(dst, src[:, n % ring], f32(hi), ALU.subtract).then_inc(done, 1)

            def stats(tt, wait_sem, wait_value):
                dve.wait_ge(wait_sem, wait_value)
                n = tal["y_sum"].next()
                nc.vector.bn_stats(ST[:, tt], Y[:, tt]).then_inc(y_sum, 1)
                dve.wait_ge(y_sum, tal["y_sum"].done(n))
                gate()
                nc.vector.bn_aggr(MV[:, tt], ST[:, tt]).then_inc(mv_ready, 1)

            def normalise(tt):
                n = tal["rstd"].next()
                i = tal["gain"].next()
                m = tal["mv"].next()
                dve.wait_ge(mv_ready, tal["mv"].done(m))
                nc.vector.scalar_tensor_tensor(out=Y[:, tt], in0=Y[:, tt], scalar=MV[:, tt, 0:1], in1=ROWS[:, 1],
                                               op0=ALU.subtract, op1=ALU.mult).then_inc(y_gain, 1)
                dve.wait_ge(rstd, tal["rstd"].done(n))
                dve.wait_ge(y_gain, tal["gain"].done(i))
                nc.vector.scalar_tensor_tensor(out=Y[:, tt], in0=Y[:, tt], scalar=RD[:, tt:tt + 1], in1=ROWS[:, 2],
                                               op0=ALU.mult, op1=ALU.add).then_inc(y_done, 1)

            rows_seen = 16
            for st in STAGES:
                dk = st.dk
                new_stage(tal, st)
                for b in range(4):
                    for kt in range(KT):
                        split_lo(w_part(b, 1)[:, kt], w_part(b, 0)[:, kt], RAW, 8, "w_hi", w_hi, w_lo)
                if st.rows:
                    rows_seen += 16 * (3 if st.cols != "ZERO" else 2)
                    dve.wait_ge(rows_full, rows_seen)
                if st.bias == "mask":
                    for qt in range(NT):
                        i = tal["side"].next()
                        dve.wait_ge(side_full[qt], tal["side"].done(i))
                        nc.vector.tensor_scalar(FB[:, qt], FB[:, qt].bitcast(I32), 0.0, -FILL, ALU.is_equal,
                                                ALU.mult).then_inc(conv_done, 1)
                    dve.wait_ge(conv_done, NT)
                    gate()

                def largest(k):
                    n = tal["s"].next()
                    if st.bias == "side" and k < NT:
                        i = tal["side_ready"].marked(k)
                        dve.wait_ge(side_ready, tal["side_ready"].done(i))
                    dve.wait_ge(s_full, tal["s"].done(n))
                    if st.bias:
                        gate()
                        nc.vector.tensor_tensor_reduce(
                            out=PR[:, k % 4], in0=psS[:, n % 2], in1=FB[:, k % NT], scale=-st.scale, scalar=BIG,
                            op0=ALU.add, op1=ALU.min, accum_out=MN[:, k % 8:k % 8 + 1]).then_inc(s_evac, 1)
                    else:
                        nc.vector.tensor_scalar(PR[:, k % 4], psS[:, n % 2], -st.scale, None, ALU.mult, ALU.min,
                                                accum_out=MN[:, k % 8:k % 8 + 1]).then_inc(s_evac, 1)

                def projection_lo(name):
                    n = tal["j"].next()
                    tal["j_own"].next()
                    i = tal["j_hi"].next()
                    kind, g = name[0], name[1]
                    dve.wait_ge(j_hi, tal["j_hi"].done(i))
                    if kind in "QK":
                        col, qk = bias_col(st, kind, g), 2 * "QK".index(kind)
                        nc.vector.scalar_tensor_tensor(
                            out=QK[:, qk + 1], in0=psJ[:, n % 2], scalar=COLS[:, col:col + 1], in1=f32(QK[:, qk]),
                            op0=ALU.add, op1=ALU.subtract).then_inc(j_evac, 1)
                    else:
                        nc.vector.tensor_tensor(value_part(st, name, 1), projected(st, n), f32(value_part(st, name, 0)),
                                                ALU.subtract).then_inc(j_evac, 1)

                def head_sum(h):
                    j = h % st.per_group
                    n = tal["pv_half"].next()
                    og = OG[j * dk:(j + 1) * dk, :]
                    dve.wait_ge(pv_half, tal["pv_half"].done(n))
                    nc.vector.tensor_tensor(og, psV[0:dk], og, ALU.add).then_inc(pv_evac, 1)

                def group_lo(g):
                    i = tal["o_hi"].next()
                    col = bias_col(st, "V", g)
                    dve.wait_ge(o_hi, tal["o_hi"].done(i))
                    nc.vector.scalar_tensor_tensor(
                        out=OT[:, 1, g], in0=OG[:, :], scalar=COLS[:, col:col + 1], in1=f32(OT[:, 0, g]),
                        op0=ALU.add, op1=ALU.subtract).then_inc(o_lo, 1)

                def out_sum(tt):
                    n = tal["j"].next()
                    tal["j_own"].next()
                    tal["j_own"].mark(tt)
                    i = tal["y"].next()
                    dve.wait_ge(j_full, tal["j"].done(n))
                    if st.cols != "ZERO":
                        m = tal["res"].next()
                        dve.wait_ge(res_ready, tal["res"].done(m))
                    else:
                        dve.wait_ge(y_full[tt], tal["y"].done(i))
                    nc.vector.tensor_tensor(Y[:, tt], psJ[:, n % 2], Y[:, tt], ALU.add).then_inc(j_evac, 1)

                def run(steps, batch):
                    for step, k, _ in steps:
                        if step == "P_LO":
                            h, qt = divmod(k, NT)
                            n = tal["t"].next()
                            i = tal["t_hi"].next()
                            dve.wait_ge(t_hi, tal["t_hi"].done(i))
                            hi, lo = (PT[h % 2][:, p, :, qt * P:(qt + 1) * P] for p in range(2))
                            nc.vector.tensor_tensor(lo, turned(st, k).rearrange("p (k t) -> p k t", k=NT), f32(hi),
                                                    ALU.subtract).then_inc(t_evac, 1)
                        elif step == "X_LO":
                            tal["j_own"].next()
                            x_lo_part(k, psJ, "j", j_evac)
                        elif step == "PROB":
                            n = tal["exp"].next()
                            dve.wait_ge(exp_done, tal["exp"].done(n))
                            nc.vector.reciprocal(RS[:, k % 8:k % 8 + 1], SM[:, k % 8:k % 8 + 1]).then_inc(recip_done, 1)
                        elif step == "SIDE":
                            i = tal["side"].next()
                            tal["side_ready"].next()
                            tal["side_ready"].mark(k)
                            dve.wait_ge(side_full[k], tal["side"].done(i))
                            if k == 0:
                                dve.wait_ge(mask_ready, tal["mask_ready"].done(tal["mask_ready"].n - 1))
                            nc.vector.scalar_tensor_tensor(out=FB[:, k], in0=FB[:, k], scalar=1.0 / st.scale, in1=ROWS[:, 0],
                                                           op0=ALU.mult, op1=ALU.add).then_inc(side_ready, 1)
                        elif step == "MAX":
                            largest(k)
                        elif step == "HEAD_SUM":
                            head_sum(k)
                        elif step == "GROUP_LO":
                            group_lo(k)
                        elif step == "J_LO":
                            projection_lo(k)
                        elif step == "C_LO":
                            split_lo(cT[:, 1, k], cT[:, 0, k], cs, 2, "cs_hi", cs_hi, cs_lo)
                        elif step == "OUT_SUM":
                            out_sum(k)
                        elif step == "STATS":
                            stats(k, j_evac, tal["j_own"].done(tal["j_own"].marked(k)))
                        elif step == "NORM":
                            if st.norm:
                                normalise(k)
                            else:
                                dve.wait_ge(j_evac, tal["j_own"].done(tal["j_own"].marked(k)))
                                dve.sem_inc(y_norm, 1)
                        elif step == "ROWMASK":
                            i = tal["mask"].next()
                            tal["mask_ready"].next()
                            dve.wait_ge(mask_full, tal["mask"].done(i))
                            nc.vector.tensor_scalar(ROWS[:, 0], ROWS[:, 0].bitcast(I32), 0.0, -FILL, ALU.is_equal,
                                                    ALU.mult).then_inc(mask_ready, 1)

                stage_loop(dve, tal, st, ["x_hi", "s", "exp", "t_hi", "t", "pv_half", "o_hi", "j", "j_hi", "j_own", "y"],
                           run)

            tal.update(h=Tally(h_full, credit=2), used=Tally(h_used, credit=4), hi=Tally(h_hi))
            acc = [psJ[:, 0], psJ[:, 1], psV[:, :], psT[:, 2]]
            for b in range(8):
                for kt in range(KT):
                    split_lo(w_part(b, 1)[:, kt], w_part(b, 0)[:, kt], RAW, 8, "w_hi", w_hi, w_lo)

            rows_seen += 48
            dve.wait_ge(rows_full, rows_seen)

            def hidden(f):
                n = tal["h"].next()
                i = tal["used"].next()
                m = tal["hi"].next()
                dve.wait_ge(h_full, tal["h"].done(n))
                dve.wait_ge(h_used, tal["used"].done(i - 4))
                nc.vector.tensor_copy(HH[:, n % 4], HF[:, n % 4]).then_inc(h_hi, 1)
                dve.wait_ge(h_hi, tal["hi"].done(m))
                nc.vector.tensor_tensor(HL[:, n % 4], HF[:, n % 4], f32(HH[:, n % 4]), ALU.subtract).then_inc(h_lo, 1)

            def sums():
                dve.wait_ge(h_used, tal["used"].done(tal["used"].n - 1))
                for tt in range(NT):
                    m = tal["res"].next()
                    tal["acc_own"].next()
                    tal["acc_own"].mark(tt)
                    dve.wait_ge(res_ready, tal["res"].done(m))
                    nc.vector.tensor_tensor(Y[:, tt], acc[tt], Y[:, tt], ALU.add).then_inc(acc_evac, 1)

            def statistics(tt):
                stats(tt, acc_evac, tal["acc_own"].done(tal["acc_own"].marked(tt)))

            def batch(prev, nxt):
                for f in range(NF):
                    hidden(f)
                    if prev and 1 <= f < 1 + NT:
                        statistics(f - 1)
                    if prev and 6 <= f < 6 + NT:
                        normalise(f - 6)
                if nxt:
                    for tt in range(NT):
                        x_lo_part(tt)
                sums()

            for tt in range(NT):
                x_lo_part(tt)
            batch(False, True)
            per = dict(x_hi=NT, t=NT, h=NF, used=NF, hi=NF, res=NT, acc_own=NT, rstd=NT, y_sum=NT, mv=NT, gain=NT)
            with turns(dve, B - 2, [(tal[k], per[k]) for k in per]):
                batch(True, True)
            batch(True, False)
            for tt in range(NT):
                statistics(tt)
            for tt in range(NT):
                normalise(tt)

        @block.gpsimd
        def _(pool):
            tal = dict(recip=Tally(recip_done), y=RingTally(y_full), mv=Tally(mv_ready), var=Tally(var_eps),
                       j=Tally(j_evac, credit=2), s=Tally(s_full), p=Tally(p_ready), pieces=Tally(stacked),
                       res=Tally(res_ready), rstd=Tally(rstd))
            last_op = [None]

            def settle(shifts):
                sems = dict(p=p_ready, pieces=stacked, res=res_ready, rstd=rstd)
                if last_op[0] and (shifts or last_op[0] == "pieces"):
                    own = tal[last_op[0]]
                    pool.wait_ge(sems[last_op[0]], own.done(own.n - 1))

            def issued(which):
                last_op[0] = which
                tal[which].next()

            nc.gpsimd.memset(ID[:, :], 0.0).then_inc(ident_zero, 1)
            pool.wait_ge(ident_zero, 1)
            nc.gpsimd.affine_select(out=ID[:, :], in_=ID[:, :], compare_op=ALU.not_equal, fill=1.0, base=0,
                                    pattern=[[-1, P]], channel_multiplier=1).then_inc(ident_ready, 1)
            pool.wait_ge(const_ready, CONSTS)

            def gate():
                pool.sem_inc(gate_pool, 1)

            def residual(tt):
                i = tal["y"].next()
                settle(False)
                pool.wait_ge(y_full[tt], tal["y"].done(i))
                issued("res")
                nc.gpsimd.tensor_tensor(Y[:, tt], Y[:, tt], ROWS[:, 0], ALU.add).then_inc(res_ready, 1)

            def deviation(tt, eps):
                n = tal["mv"].next()
                i = tal["var"].next()
                settle(False)
                pool.wait_ge(mv_ready, tal["mv"].done(n))
                nc.gpsimd.tensor_tensor(VE[:, tt:tt + 1], MV[:, tt, 1:2], CONST[:, EPS[eps]:EPS[eps] + 1],
                                        ALU.add).then_inc(var_eps, 1)
                pool.wait_ge(var_eps, tal["var"].done(i))
                issued("rstd")
                nc.gpsimd.tensor_tensor(RD[:, tt:tt + 1], VE[:, tt:tt + 1], CONST[:, 0:1], ALU.pow).then_inc(rstd, 1)

            rows_seen = 16
            for st in STAGES:
                new_stage(tal, st)
                if st.rows:
                    rows_seen += 16 * (3 if st.cols != "ZERO" else 2)
                    pool.wait_ge(rows_full, rows_seen)

                def stack_piece(h, piece):
                    if piece == 0:
                        if h % st.per_group == 0:
                            split = tal["j"].marked(("K", h // st.per_group))
                            pool.wait_ge(j_evac, tal["j"].done(split))
                        used = tal["s"].marked((h - 2) % st.heads * NT + NT - 1)
                        if used is not None:
                            pool.wait_ge(s_full, tal["s"].done(used))
                    settle(True)
                    gate()
                    issued("pieces")
                    dk, j = st.dk, h % st.per_group
                    src = f32(QK[j * dk:(j + 1) * dk])
                    dst = QS[:, h % 2]
                    pair = [src[:, 0:3:2], src[:, 1:3], src[:, 3] if dk == 64 else src[:, 0:4:3]][piece]
                    to = dst[0:dk, 2] if dk == 64 and piece == 2 else dst[piece * dk:(piece + 1) * dk, 0:2]
                    nc.gpsimd.tensor_scalar(to, pair, 1.0, 1.0, ALU.mult, ALU.mult).then_inc(stacked, 1)

                def run(steps, batch):
                    for step, k, _ in steps:
                        if step == "SCORE":
                            tal["s"].next()
                            tal["s"].mark(k)
                        elif step in ("J_LO", "X_LO", "OUT_SUM"):
                            tal["j"].next()
                            tal["j"].mark(k)
                        elif step == "STACK":
                            stack_piece(*k)
                        elif step == "PROB":
                            n = tal["recip"].next()
                            settle(False)
                            pool.wait_ge(recip_done, tal["recip"].done(n))
                            gate()
                            issued("p")
                            nc.gpsimd.tensor_scalar(PR[:, k % 4], PR[:, k % 4], RS[:, k % 8:k % 8 + 1], 1.0, ALU.mult,
                                                    ALU.mult).then_inc(p_ready, 1)
                        elif step == "RES" and st.cols != "ZERO":
                            residual(k)
                        elif step == "VAR" and st.norm:
                            deviation(k, st.eps)

                stage_loop(pool, tal, st, ["recip", "j", "s", "p", "pieces"] + (["y"] if st.cols != "ZERO" else []), run)
                if st.cols == "ZERO":
                    tal["y"].n += B * NT

            rows_seen += 48
            pool.wait_ge(rows_full, rows_seen)
            for tt in range(NT):
                residual(tt)
            with turns(pool, B - 1, [(tal[k], NT) for k in ("y", "mv", "var", "res", "rstd")]):
                for tt in range(NT):
                    deviation(tt, FF_EPS)
                for tt in range(NT):
                    residual(tt)
            for tt in range(NT):
                deviation(tt, FF_EPS)


def kernel(**inputs):
    import numpy as np
    import concourse.bacc as bacc
    from concourse import mybir
    from concourse.bass_utils import run_bass_kernel_spmd

    a = {k: np.asarray(v) for k, v in inputs.items()}
    h = AD
    l0 = lambda k: a["L0_xattn_" + k]
    l1 = lambda k: a["L1_xattn_" + k]
    blocks = []
    for half in range(2):
        cut = slice(half * h, (half + 1) * h)
        blocks += [l0("w_q")[:, cut], l0("w_k")[:, cut], l0("w_v")[:, cut], l0("w_o")[cut, :]]
    for p in ("sa", "ca"):
        blocks += [l1(f"{p}_w{m}").T for m in "qkvo"]
    blocks += [l1("ff_w1")[i * 512:(i + 1) * 512, :].T for i in range(FF // 512)]
    blocks += [l1("ff_w2")[:, i * 512:(i + 1) * 512].T for i in range(FF // 512)]
    columns = lambda v: v.reshape(-1, P).T
    arrays = {
        "x": a["x"],
        "ctx_t": a["ctx_1024"].transpose(0, 2, 1),
        "side": a["fside_Bx1xSxS2_0"],
        "key_mask": a["mask_Bx1x1xS2_ik0"].reshape(B, 1, 1, S),
        "pair_mask": a["mask_1x1xSxS_ik0"],
        "w": np.stack(blocks),
        "rows": np.stack([
            np.stack([l0("ln_b"), l0("ln_g"), l0("ln_b")]),
            np.stack([l1("sa_bo"), l1("ln1_g"), l1("ln1_b")]),
            np.stack([l1("ca_bo"), l1("ln2_g"), l1("ln2_b")]),
            np.stack([l1("ff_b2"), l1("ln3_g"), l1("ln3_b")])]),
        "cols": np.concatenate([columns(l1(f"{p}_b{m}")) for p in ("sa", "ca") for m in "qkv"]
                               + [columns(l1("ff_b1"))], axis=1),
    }
    nc = bacc.Bacc("TRN2", target_bir_lowering=False, num_devices=1, dynamic_dma_scratch_size=1024)
    feed, aps = {}, []
    for name, v in arrays.items():
        v = np.ascontiguousarray(v)
        feed[f"in_{name}"] = v
        aps.append(nc.dram_tensor(f"in_{name}", v.shape, mybir.dt.from_np(v.dtype), kind="ExternalInput").ap())
    out = nc.dram_tensor("result", (B, S, D), mybir.dt.float32, kind="ExternalOutput").ap()
    build(nc, *aps, out)
    r = run_bass_kernel_spmd(nc, [feed], core_ids=[0])
    return r.results[0]["result"]
```
